# Optimizing a Trainium2 kernel written in Bass

```python
import numpy as np
import jax
import jax.numpy as jnp

def _softmax(x, axis=-1):
    return jax.nn.softmax(x, axis=axis)

def _gelu(x):
    return jax.nn.gelu(x, approximate=True)

def _silu(x):
    return jax.nn.silu(x)

def _sigmoid(x):
    return jax.nn.sigmoid(x)

def _layernorm(x, axis=-1, eps=1e-05):
    m = jnp.mean(x, axis=axis, keepdims=True)
    v = jnp.var(x, axis=axis, keepdims=True)
    return (x - m) / jnp.sqrt(v + eps)

def _scatter_add(tgt, idx, src, axis=0):
    return tgt.at[idx].add(src)

def _segment_sum(src, seg, n):
    return jax.ops.segment_sum(src, seg, n)
kernel_name = 'mk_recurrent_d1_jaxref_r8_af526f'

def setup_inputs(seed: int=0):
    np.random.seed(seed)
    _w = jnp.asarray

    def _L0_attn_setup():
        import jax, jax.numpy as jnp
        import numpy as np
        B_SZ, T, D_MODEL, N_STATE = (4, 512, 128, 32)
        D_FF = (int(8 / 3 * D_MODEL) + 7) // 8 * 8
        EPS = 1e-06

        def _rmsnorm(x, w):
            rms = jnp.sqrt(jnp.mean(x * x, axis=-1, keepdims=True) + EPS)
            return x / rms * w
        key = jax.random.key(seed)
        ks = jax.random.split(key, 8)
        return {'x': jax.random.normal(ks[0], (B_SZ, T, D_MODEL), dtype=jnp.float32), 'log_lambda': jax.random.normal(ks[1], (N_STATE,), dtype=jnp.float32) * 0.5 + 3.0, 'B_w': jax.random.normal(ks[2], (N_STATE, D_MODEL), dtype=jnp.float32) / np.sqrt(D_MODEL), 'C_w': jax.random.normal(ks[3], (D_MODEL, N_STATE), dtype=jnp.float32) / np.sqrt(N_STATE), 'D_skip': jnp.zeros((D_MODEL,), dtype=jnp.float32), 'ssm_norm_w': jnp.ones((D_MODEL,), dtype=jnp.float32), 'ffn_norm_w': jnp.ones((D_MODEL,), dtype=jnp.float32), 'w1': jax.random.normal(ks[4], (D_FF, D_MODEL), dtype=jnp.float32) / np.sqrt(D_MODEL), 'w2': jax.random.normal(ks[5], (D_MODEL, D_FF), dtype=jnp.float32) / np.sqrt(D_FF), 'w3': jax.random.normal(ks[6], (D_FF, D_MODEL), dtype=jnp.float32) / np.sqrt(D_MODEL)}
    _L0_attn_in = _L0_attn_setup()

    def _L0_ffn_setup():
        import jax, jax.numpy as jnp
        import numpy as np
        E = 8
        D = 128
        H = 256
        TOP_K = 2
        key = jax.random.key(seed)
        k_x, k_g, k_w1, k_w2 = jax.random.split(key, 4)
        B, S = (4, 256)
        inp = {'input': jax.random.normal(k_x, (B, S, D), dtype=jnp.float32), 'Wg': jax.random.normal(k_g, (D, E), dtype=jnp.float32) * 0.02, 'W1': jax.random.normal(k_w1, (E, D, H), dtype=jnp.float32) * 0.02, 'b1': jnp.zeros((E, H), dtype=jnp.float32), 'W2': jax.random.normal(k_w2, (E, H, D), dtype=jnp.float32) * 0.02, 'b2': jnp.zeros((E, D), dtype=jnp.float32)}
        return inp
    _L0_ffn_in = _L0_ffn_setup()
    _d = {'L0_attn_x': _L0_attn_in['x'], 'L0_attn_log_lambda': _L0_attn_in['log_lambda'], 'L0_attn_B_w': _L0_attn_in['B_w'], 'L0_attn_C_w': _L0_attn_in['C_w'], 'L0_attn_D_skip': _L0_attn_in['D_skip'], 'L0_attn_ssm_norm_w': _L0_attn_in['ssm_norm_w'], 'L0_attn_ffn_norm_w': _L0_attn_in['ffn_norm_w'], 'L0_attn_w1': _L0_attn_in['w1'], 'L0_attn_w2': _L0_attn_in['w2'], 'L0_attn_w3': _L0_attn_in['w3'], 'L0_ffn_Wg': _L0_ffn_in['Wg'], 'L0_ffn_W1': _L0_ffn_in['W1'], 'L0_ffn_b1': _L0_ffn_in['b1'], 'L0_ffn_W2': _L0_ffn_in['W2'], 'L0_ffn_b2': _L0_ffn_in['b2']}
    _x0 = _d['L0_attn_x']
    _d['L0_attn_x'] = jax.random.normal(jax.random.fold_in(jax.random.key(seed), 1), (16, 512, 128), dtype=_x0.dtype)
    del _x0
    return _d

def reference(L0_attn_x, L0_attn_log_lambda, L0_attn_B_w, L0_attn_C_w, L0_attn_D_skip, L0_attn_ssm_norm_w, L0_attn_ffn_norm_w, L0_attn_w1, L0_attn_w2, L0_attn_w3, L0_ffn_Wg, L0_ffn_W1, L0_ffn_b1, L0_ffn_W2, L0_ffn_b2):

    def _L0_attn_ref(x, log_lambda, B_w, C_w, D_skip, ssm_norm_w, ffn_norm_w, w1, w2, w3):
        import jax, jax.numpy as jnp
        import numpy as np
        B_SZ, T, D_MODEL, N_STATE = (4, 512, 128, 32)
        D_FF = (int(8 / 3 * D_MODEL) + 7) // 8 * 8
        EPS = 1e-06

        def _rmsnorm(x, w):
            rms = jnp.sqrt(jnp.mean(x * x, axis=-1, keepdims=True) + EPS)
            return x / rms * w
        u = _rmsnorm(x, ssm_norm_w)
        lam = jax.nn.sigmoid(log_lambda)
        Bu = jnp.einsum('btd,nd->btn', u, B_w)

        def step(h, bu_t):
            h = lam * h + bu_t
            return (h, h)
        h0 = jnp.zeros((x.shape[0], log_lambda.shape[0]), dtype=x.dtype)
        _, hs = jax.lax.scan(step, h0, jnp.swapaxes(Bu, 0, 1))
        hs = jnp.swapaxes(hs, 0, 1)
        y = jnp.einsum('btn,dn->btd', hs, C_w) + D_skip * u
        x = x + y
        z = _rmsnorm(x, ffn_norm_w)
        gate = jax.nn.silu(jnp.einsum('btd,fd->btf', z, w1))
        val = jnp.einsum('btd,fd->btf', z, w3)
        ffn = jnp.einsum('btf,df->btd', gate * val, w2)
        return x + ffn

    def _L0_ffn_ref(input, Wg, W1, b1, W2, b2):
        import jax, jax.numpy as jnp
        import numpy as np
        E = 8
        D = 128
        H = 256
        TOP_K = 2
        logits = jnp.einsum('bsd,de->bse', input, Wg)
        probs = jax.nn.softmax(logits, axis=-1)
        top_vals, top_idx = jax.lax.top_k(probs, TOP_K)
        top_vals = top_vals / jnp.sum(top_vals, axis=-1, keepdims=True)
        onehot = jax.nn.one_hot(top_idx, E, dtype=input.dtype)
        mask = jnp.sum(onehot, axis=2)
        scores = jnp.sum(onehot * top_vals[..., None], axis=2)
        xm = input[None] * jnp.moveaxis(mask, -1, 0)[..., None]
        h = jnp.einsum('ebsd,edh->ebsh', xm, W1) + b1[:, None, None, :]
        h = jax.nn.relu(h)
        y = jnp.einsum('ebsh,ehd->ebsd', h, W2) + b2[:, None, None, :]
        out = jnp.sum(y * jnp.moveaxis(scores, -1, 0)[..., None], axis=0)
        return out
    x = L0_attn_x
    xn = _layernorm(x, axis=-1)
    s = _L0_attn_ref(xn, L0_attn_log_lambda, L0_attn_B_w, L0_attn_C_w, L0_attn_D_skip, L0_attn_ssm_norm_w, L0_attn_ffn_norm_w, L0_attn_w1, L0_attn_w2, L0_attn_w3)
    g = _silu(_L0_ffn_ref(xn, L0_ffn_Wg, L0_ffn_W1, L0_ffn_b1, L0_ffn_W2, L0_ffn_b2))
    x = x + s * g
    return x

_drawn_inputs = setup_inputs


def setup_inputs(seed=0):
    import zlib

    import numpy as np

    out = dict(_drawn_inputs(seed))
    spreads = {'L0_attn_D_skip': (0.0, 0.8),
     'L0_attn_ssm_norm_w': (1.0, 0.6),
     'L0_attn_ffn_norm_w': (1.0, 0.6),
     'L0_ffn_b1': (0.0, 0.313),
     'L0_ffn_b2': (0.0, 0.1)}
    factors = {}
    for name, (base, spread) in spreads.items():
        noise = np.random.default_rng([zlib.crc32(name.encode()), seed]).standard_normal(out[name].shape)
        drawn = base * np.exp(spread * noise) if base else spread * noise
        out[name] = jnp.asarray(drawn.astype(out[name].dtype))
    for name, factor in factors.items():
        out[name] = (out[name] * factor).astype(out[name].dtype)
    return out
```

```python
from collections import namedtuple
from contextlib import ExitStack

import concourse.bass as bass
from concourse import mybir

P = 128
D = 128
B = 16
T = 512
TT = T // P
NS = 32
FF = 344
FC = (FF + P - 1) // P
E = 8
H = 256
HC = H // P
ES = E * HC
SLOTS = ES + 2 * FC
YS = E + 1
AHEAD = 3
FIRST = AHEAD + 1
STEPS = 6
LN_EPS = 1e-5
RMS_EPS = 1e-6

F32 = mybir.dt.float32
F32R = mybir.dt.float32r
U32 = mybir.dt.uint32
ALU = mybir.AluOpType
ACT = mybir.ActivationFunctionType

Group = namedtuple("Group", "n half parity")


def after(g):
    return Group(g.n + 1, g.half + g.parity, 1 - g.parity)


def hidden_rows(s):
    return P if s < ES else min(P, FF - (s - ES) // 2 * P)


def build(nc, x, log_lambda, B_w, C_w, D_skip, ssm_norm_w, ffn_norm_w, w1, w2, w3, Wg, W1, b1, W2, b2, out):
    x_v = x.rearrange("b (j p) d -> b p j d", p=P)
    out_v = out.rearrange("b (j p) d -> b p j d", p=P)

    with ExitStack() as ctx:
        def sb(name, shape, dt=F32):
            return ctx.enter_context(nc.sbuf_tensor(name, shape, dt))

        def psum(name, shape):
            return ctx.enter_context(nc.psum_tensor(name, shape, F32))

        def sem(name):
            return ctx.enter_context(nc.semaphore(name))

        W1_raw = sb("W1_raw", [P, E, H])
        W1_row0 = sb("W1_row0", [P, E, H])
        W2_raw = sb("W2_raw", [P, E, HC, D])
        Wg_raw = sb("Wg_raw", [P, E])
        Wg_row0 = sb("Wg_row0", [P, E])
        w1_raw = sb("w1_raw", [P, FC, D])
        w3_raw = sb("w3_raw", [P, FC, D])
        w2_raw = sb("w2_raw", [P, FF])
        Bw_raw = sb("Bw_raw", [NS, D])
        Cw_raw = sb("Cw_raw", [D, NS])
        vec_rows = sb("vec_rows", [E + 3, D])
        log_lam = sb("log_lam", [NS, 1])
        W1_hi, W1_lo = sb("W1_hi", [P, E, H], F32R), sb("W1_lo", [P, E, H], F32R)
        W2_hi, W2_lo = sb("W2_hi", [P, E, HC, D], F32R), sb("W2_lo", [P, E, HC, D], F32R)
        Wg_parts = sb("Wg_parts", [P, 2, E], F32R)
        w1T, w3T = sb("w1T", [P, FF]), sb("w3T", [P, FF])
        w13T = [w1T, w3T]
        w13T_hi = [sb("w1T_hi", [P, FF], F32R), sb("w3T_hi", [P, FF], F32R)]
        w13T_lo = [sb("w1T_lo", [P, FF], F32R), sb("w3T_lo", [P, FF], F32R)]
        w2T = sb("w2T", [P, FC, D])
        w2T_hi, w2T_lo = sb("w2T_hi", [P, FC, D], F32R), sb("w2T_lo", [P, FC, D], F32R)
        BT = sb("BT", [P, P])
        BT_hi, BT_lo = sb("BT_hi", [P, P], F32R), sb("BT_lo", [P, P], F32R)
        CT = sb("CT", [NS, D])
        C_stack = sb("C_stack", [3 * NS, D], F32R)
        vecT = sb("vecT", [P, E + 3])
        D_w = sb("D_w", [P, 1])
        lam_tanh, lam = sb("lam_tanh", [NS, 1]), sb("lam", [NS, 1])
        lam_b = sb("lam_b", [NS, T])
        ident = sb("ident", [P, P])
        ones = sb("ones", [P, 1])
        warm = sb("warm", [P, 1])
        minus_half = sb("minus_half", [P, TT])
        expert_no = sb("expert_no", [P, TT, E])
        x_all = sb("x_all", [P, B, TT, D])
        bn = sb("bn", [P, TT, 6])
        shift = sb("shift", [P, TT])
        mean_sum, mean_gap, square_sum = sb("mean_sum", [P, TT]), sb("mean_gap", [P, TT]), sb("square_sum", [P, TT])
        mean, gap_square, var = sb("mean", [P, TT]), sb("gap_square", [P, TT]), sb("var", [P, TT])
        var_eps, rstd = sb("var_eps", [P, TT]), sb("rstd", [P, TT])
        rstd2, msq, msq_eps, rrms = sb("rstd2", [P, TT]), sb("msq", [P, TT]), sb("msq_eps", [P, TT]), sb("rrms", [P, TT])
        xn_tok, u_tok = sb("xn_tok", [P, TT, D]), sb("u_tok", [P, TT, D])
        xn_hi = [sb(f"xn_hi{i}", [P, T], F32R) for i in range(2)]
        xn_lo = [sb(f"xn_lo{i}", [P, T], F32R) for i in range(2)]
        u_hi, u_lo = sb("u_hi", [P, T], F32R), sb("u_lo", [P, T], F32R)
        du, base = sb("du", [P, T]), sb("base", [P, T])
        logits = sb("logits", [P, TT, E])
        top, top_i = sb("top", [P, TT, 8]), sb("top_i", [P, TT, 8], U32)
        gap, gap_tanh = sb("gap", [P, TT]), sb("gap_tanh", [P, TT])
        score = [sb(f"score{k}", [P, TT]) for k in range(2)]
        chosen = [sb(f"chosen{k}", [P, TT, E]) for k in range(2)]
        part = [sb(f"part{k}", [P, TT, E]) for k in range(2)]
        s_tok = sb("s_tok", [P, TT, E])
        s_row = sb("s_row", [E, T])
        s_b = [sb(f"s_b{i}", [P, T]) for i in range(4)]
        hs = sb("hs", [NS, T])
        hs_stack = sb("hs_stack", [3 * NS, T], F32R)
        x1 = [sb(f"x1_{i}", [P, T]) for i in range(2)]
        x1_sq = sb("x1_sq", [P, T])
        z_msq, z_r = sb("z_msq", [P, TT]), sb("z_r", [P, TT])
        r_row, r_b = sb("r_row", [1, T]), sb("r_b", [P, T])
        z = sb("z", [P, T])
        z_hi, z_lo = sb("z_hi", [P, T], F32R), sb("z_lo", [P, T], F32R)
        h_hi = [sb(f"h_hi{i}", [P, T], F32R) for i in range(4)]
        h_lo = [sb(f"h_lo{i}", [P, T], F32R) for i in range(4)]
        gate, gv = sb("gate", [P, T]), [sb(f"gv{i}", [P, T]) for i in range(2)]
        ys = [sb(f"ys{i}", [P, T]) for i in range(2)]
        moe, moe_silu = sb("moe", [P, T]), sb("moe_silu", [P, T])
        s_sum, sg = sb("s_sum", [P, T]), sb("sg", [P, T])

        hid = [psum(f"hid{i}", [P, T]) for i in range(4)]
        y = [psum(f"y{i}", [P, T]) for i in range(2)]
        m0, m1 = psum("m0", [P, T]), psum("m1", [P, T])

        x_loaded = [sem("x_even_loaded"), sem("x_odd_loaded")]
        small_loaded, ffn_loaded = sem("small_loaded"), sem("ffn_loaded")
        W1_loaded, b1_loaded, W2_loaded = sem("W1_loaded"), sem("b1_loaded"), sem("W2_loaded")
        stored = sem("stored")
        pool_consts, dve_consts, ident_made = sem("pool_consts"), sem("dve_consts"), sem("ident_made")
        lam_done, wt_t = sem("lam_done"), sem("wt_t")
        small_wt, small_hi, small_lo = sem("small_wt"), sem("small_hi"), sem("small_lo")
        ffn_wt, ffn_hi, ffn_lo = sem("ffn_wt"), sem("ffn_hi"), sem("ffn_lo")
        W1_shift, W1_hi_done, W1_lo_done = sem("W1_shift"), sem("W1_hi_done"), sem("W1_lo_done")
        W2_hi_done, W2_lo_done = sem("W2_hi_done"), sem("W2_lo_done")
        stats_step = sem("stats_step")
        var_done, shift_done, msq_done = sem("var_done"), sem("shift_done"), sem("msq_done")
        rstd_done, rrms_done = sem("rstd_done"), sem("rrms_done")
        xn_tok_done, u_tok_done = sem("xn_tok_done"), sem("u_tok_done")
        xn_t, u_t = sem("xn_t"), sem("u_t")
        xn_hi_done, du_done = sem("xn_hi_done"), sem("du_done")
        xn_lo_done, u_lo_done, base_done = sem("xn_lo_done"), sem("u_lo_done"), sem("base_done")
        bias_row = sem("bias_row")
        logits_mm, bu_mm, s_t = sem("logits_mm"), sem("bu_mm"), sem("s_t")
        route_step, gap_done, s_tok_done = sem("route_step"), sem("gap_done"), sem("s_tok_done")
        tanh_done, s_row_done = sem("tanh_done"), sem("s_row_done")
        s_b_done = [sem(f"s_b{i}_done") for i in range(4)]
        hs_done, hs_lo_done, hs_hi_done = sem("hs_done"), sem("hs_lo_done"), sem("hs_hi_done")
        c_mm, x1_done, sq_done, ms_mm = sem("c_mm"), sem("x1_done"), sem("sq_done"), sem("ms_mm")
        z_msq_done, z_r_done, r_t, r_row_done = sem("z_msq_done"), sem("z_r_done"), sem("r_t"), sem("r_row_done")
        r_b_done, z_done, z_hi_done, z_lo_done = sem("r_b_done"), sem("z_done"), sem("z_hi_done"), sem("z_lo_done")
        hid_mm, y_mm = sem("hid_mm"), sem("y_mm")
        h_hi_done, h_lo_done = sem("h_hi_done"), sem("h_lo_done")
        gate_done, gv_done, gv_hi_done, gv_lo_done = sem("gate_done"), sem("gv_done"), sem("gv_hi_done"), sem("gv_lo_done")
        y_scaled, moe_added = sem("y_scaled"), sem("moe_added")
        moe_silu_done, s_sum_done, sg_done, sg_t, out_done = sem("moe_silu_done"), sem("s_sum_done"), sem("sg_done"), sem("sg_t"), sem("out_done")

        def bank(g, s):
            return (g.parity * SLOTS + s) % 4

        def y_bank(g, k):
            return (g.parity * YS + k) % 2

        def passed(eng, semaphore, value):
            if not isinstance(value, int) or value > 0:
                eng.wait_ge(semaphore, value)


        def iterations(eng, step):
            with eng.Fori(0, B // 2 - 1) as pair:
                step(Group(pair * 2, pair, 0), False)
                step(Group(pair * 2 + 1, pair, 1), False)
            step(Group(B - 2, B // 2 - 1, 0), False)
            step(Group(B - 1, B // 2 - 1, 1), True)

        def time_slots(g, last):
            for c in range(FIRST, SLOTS):
                yield g, c
            if not last:
                for c in range(FIRST):
                    yield after(g), c

        def ahead(g, c, by, last):
            if c + by < SLOTS:
                return g, c + by
            return None if last else (after(g), c + by - SLOTS)

        block = ctx.enter_context(nc.Block())

        @block.sync
        def _(sp):
            def load(g):
                passed(sp, x_loaded[g.parity], g.half * 16)
                sp.dma_start(x_all[:, bass.ds(g.n, 1), :, :].rearrange("p o j d -> p (o j) d"),
                             x_v[bass.ds(g.n, 1)].rearrange("o p j d -> p (o j) d")).then_inc(x_loaded[g.parity], 16)

            def broadcast_score(g, e):
                passed(sp, y_scaled, g.n * E + e - 3)
                if e == 0:
                    sp.wait_ge(s_row_done, g.n + 1)
                sp.dma_start(s_b[e % 4][:], s_row[e:e + 1, :].unsqueeze(1).to_broadcast([1, P, T])).then_inc(s_b_done[e % 4], 16)

            def broadcast_r(g):
                sp.wait_ge(r_row_done, g.n + 1)
                sp.dma_start(r_b[:], r_row[:].unsqueeze(1).to_broadcast([1, P, T])).then_inc(r_b_done, 16)

            def store(g):
                sp.wait_ge(out_done, g.n + 1)
                sp.dma_start(out_v[bass.ds(g.n, 1)].rearrange("o p j d -> p (o j) d"),
                             x_all[:, bass.ds(g.n, 1), :, :].rearrange("p o j d -> p (o j) d")).then_inc(stored, 16)

            g0 = Group(0, 0, 0)
            load(g0)
            load(after(g0))
            sp.wait_ge(W1_shift, 1)
            sp.dma_start(W1_raw[0:1], b1.rearrange("(o e) h -> o e h", o=1)).then_inc(b1_loaded, 16)
            broadcast_score(g0, 0)
            broadcast_score(g0, 1)

            def slot(g, c, last):
                if c == 5:
                    broadcast_r(g)
                if c % 2 and c + 3 < ES:
                    broadcast_score(g, (c + 3) // 2)
                if c in (19, 21) and not last:
                    broadcast_score(after(g), (c - 19) // 2)

            for c in range(FIRST):
                slot(g0, c, False)

            def step(g, last):
                if not isinstance(g.n, int):
                    load(after(after(g)))
                for gg, c in time_slots(g, last):
                    slot(gg, c, last)
                store(g)

            iterations(sp, step)
            sp.wait_ge(stored, B * 16)

        @block.gpsimd
        def _(pool):
            nc.gpsimd.memset(ident[:], 0.0).then_inc(ident_made, 1)
            pool.wait_ge(ident_made, 1)
            nc.gpsimd.affine_select(out=ident[:], in_=ident[:], compare_op=ALU.not_equal, fill=1.0, base=0,
                                    pattern=[[-1, P]], channel_multiplier=1).then_inc(ident_made, 1)
            nc.gpsimd.memset(minus_half[:], -0.5)
            nc.gpsimd.memset(ones[:], 1.0).then_inc(pool_consts, 1)
            pool.wait_ge(pool_consts, 1)

            def rstd_pow(g):
                pool.wait_ge(var_done, g.n + 1)
                nc.gpsimd.tensor_tensor(rstd[:], var_eps[:], minus_half[:], ALU.pow).then_inc(rstd_done, 1)

            def rrms_pow(g):
                pool.wait_ge(msq_done, g.n + 1)
                nc.gpsimd.tensor_tensor(rrms[:], msq_eps[:], minus_half[:], ALU.pow).then_inc(rrms_done, 1)

            def bias_rows(g):
                pool.wait_ge(pool_consts, 1)
                pool.wait_ge(xn_lo_done, g.n + 1)
                nc.gpsimd.memset(xn_hi[g.parity][0:1, :].bitcast(F32), 1.0)
                nc.gpsimd.memset(xn_lo[g.parity][0:1, :].bitcast(F32), 0.0).then_inc(bias_row, 1)

            def add_expert(g, e):
                if e >= 2:
                    pool.wait_ge(moe_added, g.n * (E - 1) + e - 1)
                pool.wait_ge(y_scaled, g.n * E + e + 1)
                nc.gpsimd.tensor_tensor(moe[:], moe[:], ys[e % 2][:], ALU.add).then_inc(moe_added, 1)

            def z_pow(g):
                pool.wait_ge(z_msq_done, g.n + 1)
                nc.gpsimd.tensor_tensor(z_r[:], z_msq[:], minus_half[:], ALU.pow).then_inc(z_r_done, 1)

            def z_scale(g):
                pool.wait_ge(r_b_done, g.n * 16 + 16)
                nc.gpsimd.tensor_tensor(z[:], x1[g.parity][:], r_b[:], ALU.mult).then_inc(z_done, 1)

            def z_low(g):
                pool.wait_ge(z_hi_done, g.n + 1)
                nc.gpsimd.tensor_tensor(z_lo[:], z[:], z_hi[:].bitcast(F32), ALU.subtract).then_inc(z_lo_done, 1)

            g0 = Group(0, 0, 0)
            rstd_pow(g0)
            rrms_pow(g0)
            bias_rows(g0)
            z_pow(g0)

            def slot(g, c, last):
                if c % 2 and 5 <= c < ES + 2:
                    add_expert(g, (c - 3) // 2)
                if c == 7:
                    z_scale(g)
                if c == 9:
                    z_low(g)
                if c >= FIRST and not last:
                    n = after(g)
                    if c == 5:
                        rstd_pow(n)
                    if c == 7:
                        rrms_pow(n)
                    if c == 12:
                        bias_rows(n)

            def step(g, last):
                for gg, c in time_slots(g, last):
                    slot(gg, c, last)
                    if c == 2:
                        z_pow(gg)

            iterations(pool, step)

        @block.scalar
        def _(act):
            act.dma_start(Wg_raw[:], Wg).then_inc(small_loaded, 16)
            act.dma_start(Wg_row0[:], Wg[0:1, :].to_broadcast([P, E])).then_inc(small_loaded, 16)
            act.dma_start(Bw_raw[:], B_w).then_inc(small_loaded, 16)
            act.dma_start(Cw_raw[:], C_w).then_inc(small_loaded, 16)
            act.dma_start(vec_rows[0:E, :], b2).then_inc(small_loaded, 16)
            for k, v in enumerate((D_skip, ssm_norm_w, ffn_norm_w)):
                act.dma_start(vec_rows[E + k:E + k + 1, :], v.rearrange("(o d) -> o d", o=1)).then_inc(small_loaded, 16)
            act.dma_start(log_lam[:], log_lambda.rearrange("(n o) -> n o", o=1)).then_inc(lam_done, 16)
            act.dma_start(W1_raw[:], W1.rearrange("e d h -> d e h")).then_inc(W1_loaded, 16)
            act.dma_start(W1_row0[:], W1[:, 0:1, :].rearrange("e d h -> d e h").to_broadcast([P, E, H])).then_inc(W1_loaded, 16)
            act.dma_start(W2_raw[:], W2.rearrange("e (c p) d -> p e c d", p=P)).then_inc(W2_loaded, 16)
            full = FF // P * P
            for w, raw in ((w1, w1_raw), (w3, w3_raw)):
                act.dma_start(raw[:, 0:FF // P, :], w[0:full, :].rearrange("(c p) d -> p c d", p=P)).then_inc(ffn_loaded, 16)
                act.dma_start(raw[0:FF - full, FC - 1, :], w[full:FF, :]).then_inc(ffn_loaded, 16)
            act.dma_start(w2_raw[:], w2).then_inc(ffn_loaded, 16)

            def xn_tokens(g):
                act.wait_ge(pool_consts, 1)
                act.wait_ge(shift_done, g.n + 1)
                for j in range(TT):
                    last = nc.scalar.activation(
                        xn_tok[:, j, :], x_all[:, bass.ds(g.n, 1), j, :].rearrange("p o d -> p (o d)"),
                        ACT.Identity, bias=shift[:, j:j + 1], scale=rstd[:, j:j + 1])
                last.then_inc(xn_tok_done, 1)

            def u_tokens(g):
                act.wait_ge(xn_tok_done, g.n + 1)
                act.wait_ge(rrms_done, g.n + 1)
                for j in range(TT):
                    last = nc.scalar.activation(u_tok[:, j, :], xn_tok[:, j, :], ACT.Copy, scale=rrms[:, j:j + 1])
                last.then_inc(u_tok_done, 1)

            def xn_high(g):
                act.wait_ge(xn_t, g.n + 1)
                nc.scalar.activation(xn_hi[g.parity][:], m0[:], ACT.Copy).then_inc(xn_hi_done, 1)

            def u_high(g):
                act.wait_ge(u_t, g.n + 1)
                nc.scalar.activation(u_hi[:], m1[:], ACT.Copy)
                nc.scalar.activation(du[:], m1[:], ACT.Copy, scale=D_w[:, 0:1]).then_inc(du_done, 1)

            def gap_to_tanh(g):
                act.wait_ge(gap_done, g.n + 1)
                nc.scalar.activation(gap_tanh[:], gap[:], ACT.Tanh, scale=0.5).then_inc(tanh_done, 1)

            def hs_high(g):
                act.wait_ge(hs_done, g.n + 1)
                nc.scalar.activation(hs_stack[0:NS, :], hs[:], ACT.Copy)
                nc.scalar.activation(hs_stack[2 * NS:3 * NS, :], hs[:], ACT.Copy).then_inc(hs_hi_done, 1)

            def score_rows(g):
                for i in range(4):
                    passed(act, s_b_done[i], g.n * (E // 4 * 16))
                act.wait_ge(s_t, g.n + 1)
                nc.scalar.activation(s_row[:], m0[0:E, :], ACT.Copy).then_inc(s_row_done, 1)

            def square(g):
                act.wait_ge(x1_done, g.n + 1)
                nc.scalar.activation(x1_sq[:], x1[g.parity][:], ACT.Square).then_inc(sq_done, 1)

            def r_rows(g):
                act.wait_ge(r_t, g.n + 1)
                nc.scalar.activation(r_row[:], m0[0:1, :], ACT.Copy).then_inc(r_row_done, 1)

            def z_high(g):
                act.wait_ge(z_done, g.n + 1)
                nc.scalar.activation(z_hi[:], z[:], ACT.Copy).then_inc(z_hi_done, 1)

            def evacuate(g, s):
                k, b = hidden_rows(s), bank(g, s)
                f = (s - ES) // 2
                if s < ES:
                    act.wait_ge(hid_mm, g.n * SLOTS + s + 1)
                    nc.scalar.activation(h_hi[b][:], hid[b][:], ACT.Relu).then_inc(h_hi_done, 1)
                elif s % 2 == 0:
                    act.wait_ge(hid_mm, g.n * SLOTS + s + 1)
                    nc.scalar.activation(gate[0:k, :], hid[b][0:k, :], ACT.Silu).then_inc(gate_done, 1)
                else:
                    act.wait_ge(gv_done, g.n * FC + f + 1)
                    nc.scalar.activation(h_hi[b][0:k, :], gv[f % 2][0:k, :], ACT.Copy).then_inc(gv_hi_done, 1)

            def moe_gate(g):
                act.wait_ge(moe_added, g.n * (E - 1) + E - 1)
                nc.scalar.activation(moe_silu[:], moe[:], ACT.Silu).then_inc(moe_silu_done, 1)

            g0 = Group(0, 0, 0)
            act.wait_ge(pool_consts, 1)
            nc.scalar.activation(warm[:], ones[:], ACT.Silu)
            act.wait_ge(lam_done, 16)
            nc.scalar.activation(lam_tanh[:], log_lam[:], ACT.Tanh, scale=0.5).then_inc(lam_done, 1)
            xn_tokens(g0)
            u_tokens(g0)
            xn_high(g0)
            act.wait_ge(small_wt, 3)
            nc.scalar.activation(Wg_parts[:, 0, :], Wg_raw[:], ACT.Copy)
            nc.scalar.activation(BT_hi[:], BT[:], ACT.Copy)
            nc.scalar.activation(C_stack[0:NS, :], CT[:], ACT.Copy)
            nc.scalar.activation(C_stack[NS:2 * NS, :], CT[:], ACT.Copy).then_inc(small_hi, 1)
            u_high(g0)
            act.wait_ge(b1_loaded, 16)
            nc.scalar.activation(W1_hi[:], W1_raw[:], ACT.Copy).then_inc(W1_hi_done, 1)
            hs_high(g0)
            gap_to_tanh(g0)
            act.wait_ge(W2_loaded, 16)
            nc.scalar.activation(W2_hi[:], W2_raw[:], ACT.Copy).then_inc(W2_hi_done, 1)
            score_rows(g0)
            square(g0)
            evacuate(g0, 0)
            evacuate(g0, 1)
            act.wait_ge(ffn_wt, 3)
            for i in range(2):
                nc.scalar.activation(w13T_hi[i][:], w13T[i][:], ACT.Copy)
            for c in range(FC):
                k = hidden_rows(ES + 2 * c)
                last = nc.scalar.activation(w2T_hi[0:k, c, :], w2T[0:k, c, :], ACT.Copy)
            last.then_inc(ffn_hi, 1)

            def slot(g, c, last):
                n = after(g) if c >= FIRST else g
                nxt = ahead(g, c, 2, last)
                if nxt:
                    evacuate(*nxt)
                if c == 5:
                    r_rows(g)
                if c == 9:
                    z_high(g)
                if c == 18:
                    moe_gate(g)
                if c >= FIRST and not last:
                    if c == 7:
                        xn_tokens(n)
                    if c == 8:
                        u_tokens(n)
                    if c == 10:
                        xn_high(n)
                    if c == 11:
                        u_high(n)
                    if c == 16:
                        hs_high(n)
                        gap_to_tanh(n)
                    if c == 19:
                        score_rows(n)

            for c in range(FIRST):
                slot(g0, c, False)

            def step(g, last):
                for gg, c in time_slots(g, last):
                    slot(gg, c, last)
                    if c == 0:
                        square(gg)

            iterations(act, step)

        @block.vector
        def _(dve):
            for e in range(E):
                nc.vector.memset(expert_no[:, :, e:e + 1], float(e))
            nc.vector.memset(BT[:], 0.0)
            nc.vector.memset(lam_b[:], 1.0)
            nc.vector.memset(C_stack[:].bitcast(F32), 0.0).then_inc(dve_consts, 1)
            dve.wait_ge(dve_consts, 1)

            def statistics(g):
                dve.wait_ge(dve_consts, 1)
                dve.wait_ge(x_loaded[g.parity], g.half * 16 + 16)
                for j in range(TT):
                    last = nc.vector.bn_stats(bn[:, j, :], x_all[:, bass.ds(g.n, 1), j, :].rearrange("p o d -> p (o d)"))
                last.then_inc(stats_step, 1)
                half = [bn[:, :, k] for k in range(6)]
                dve.wait_ge(stats_step, g.n * STEPS + 1)
                nc.vector.tensor_tensor(mean_sum[:], half[1], half[4], ALU.add)
                nc.vector.tensor_tensor(mean_gap[:], half[1], half[4], ALU.subtract)
                nc.vector.tensor_tensor(square_sum[:], half[2], half[5], ALU.add).then_inc(stats_step, 1)
                dve.wait_ge(stats_step, g.n * STEPS + 2)
                nc.vector.tensor_scalar(mean[:], mean_sum[:], 0.5, None, ALU.mult)
                nc.vector.scalar_tensor_tensor(gap_square[:], mean_gap[:], 0.25, mean_gap[:], ALU.mult,
                                               ALU.mult).then_inc(stats_step, 1)
                dve.wait_ge(stats_step, g.n * STEPS + 3)
                nc.vector.scalar_tensor_tensor(var[:], square_sum[:], 1.0 / D, gap_square[:], ALU.mult,
                                               ALU.add).then_inc(stats_step, 1)
                dve.wait_ge(stats_step, g.n * STEPS + 4)
                nc.vector.tensor_scalar(var_eps[:], var[:], LN_EPS, None, ALU.add).then_inc(var_done, 1)

            def mean_square(g):
                dve.wait_ge(rstd_done, g.n + 1)
                nc.vector.scalar_tensor_tensor(shift[:], mean[:], -1.0, rstd[:], ALU.mult, ALU.mult).then_inc(shift_done, 1)
                nc.vector.tensor_tensor(rstd2[:], rstd[:], rstd[:], ALU.mult).then_inc(stats_step, 1)
                dve.wait_ge(stats_step, g.n * STEPS + 5)
                nc.vector.tensor_tensor(msq[:], rstd2[:], var[:], ALU.mult).then_inc(stats_step, 1)
                dve.wait_ge(stats_step, g.n * STEPS + 6)
                nc.vector.tensor_scalar(msq_eps[:], msq[:], RMS_EPS, None, ALU.add).then_inc(msq_done, 1)

            def xn_low(g):
                dve.wait_ge(xn_hi_done, g.n + 1)
                nc.vector.tensor_tensor(xn_lo[g.parity][:], m0[:], xn_hi[g.parity][:].bitcast(F32),
                                        ALU.subtract).then_inc(xn_lo_done, 1)

            def u_low(g):
                dve.wait_ge(du_done, g.n + 1)
                nc.vector.tensor_tensor(u_lo[:], m1[:], u_hi[:].bitcast(F32), ALU.subtract).then_inc(u_lo_done, 1)

            def skip_sum(g):
                nc.vector.tensor_tensor(base[:], m0[:], du[:], ALU.add).then_inc(base_done, 1)

            def route_sum(g):
                dve.wait_ge(logits_mm, g.n + 1)
                nc.vector.tensor_reduce(logits[:], m0[:, 0:2 * TT * E].rearrange("p (j i e) -> p j e i", j=TT, i=2),
                                        mybir.AxisListType.X, ALU.add).then_inc(route_step, 1)

            def scan(g):
                dve.wait_ge(bu_mm, g.n + 1)
                dve.wait_ge(route_step, g.n * 6 + 1)
                nc.vector.tensor_tensor_scan(hs[:], lam_b[:], m1[0:NS, :], 0.0, ALU.mult, ALU.add).then_inc(hs_done, 1)

            def route_top(g):
                for j in range(TT):
                    last = nc.vector.max(top[:, j, :], logits[:, j, :])
                last.then_inc(route_step, 1)
                dve.wait_ge(route_step, g.n * 6 + 2)
                nc.vector.tensor_tensor(gap[:], top[:, :, 0], top[:, :, 1], ALU.subtract).then_inc(gap_done, 1)
                for j in range(TT):
                    last = nc.vector.max_index(top_i[:, j, :], top[:, j, :], logits[:, j, :])
                last.then_inc(route_step, 1)
                dve.wait_ge(route_step, g.n * 6 + 3)
                for k in range(2):
                    last = nc.vector.tensor_tensor(chosen[k][:], top_i[:, :, k:k + 1].to_broadcast([P, TT, E]),
                                                   expert_no[:], ALU.is_equal)
                last.then_inc(route_step, 1)

            def route_scores(g):
                dve.wait_ge(tanh_done, g.n + 1)
                for k, sign in enumerate((0.5, -0.5)):
                    last = nc.vector.tensor_scalar(score[k][:], gap_tanh[:], sign, 0.5, ALU.mult, ALU.add)
                last.then_inc(route_step, 1)
                dve.wait_ge(route_step, g.n * 6 + 5)
                for k in range(2):
                    last = nc.vector.tensor_tensor(part[k][:], chosen[k][:],
                                                   score[k][:].unsqueeze(2).to_broadcast([P, TT, E]), ALU.mult)
                last.then_inc(route_step, 1)
                dve.wait_ge(route_step, g.n * 6 + 6)
                nc.vector.tensor_tensor(s_tok[:], part[0][:], part[1][:], ALU.add).then_inc(s_tok_done, 1)

            def hs_low(g):
                dve.wait_ge(hs_hi_done, g.n + 1)
                nc.vector.tensor_tensor(hs_stack[NS:2 * NS, :], hs[:], hs_stack[0:NS, :].bitcast(F32),
                                        ALU.subtract).then_inc(hs_lo_done, 1)

            def first_residual(g):
                dve.wait_ge(c_mm, g.n + 1)
                nc.vector.tensor_tensor(x1[g.parity][:], m0[:], base[:], ALU.add).then_inc(x1_done, 1)

            def z_mean_square(g):
                dve.wait_ge(ms_mm, g.n + 1)
                nc.vector.tensor_scalar(z_msq[:], m0[:, 0:TT], 1.0 / D, RMS_EPS, ALU.mult, ALU.add).then_inc(z_msq_done, 1)

            def low_part(g, s):
                k, b = hidden_rows(s), bank(g, s)
                f = (s - ES) // 2
                if s < ES:
                    dve.wait_ge(h_hi_done, g.n * ES + s + 1)
                    nc.vector.scalar_tensor_tensor(h_lo[b][:], hid[b][:], 0.0, h_hi[b][:].bitcast(F32),
                                                   ALU.max, ALU.subtract).then_inc(h_lo_done, 1)
                elif s % 2:
                    dve.wait_ge(gv_hi_done, g.n * FC + f + 1)
                    nc.vector.tensor_tensor(h_lo[b][0:k, :], gv[f % 2][0:k, :], h_hi[b][0:k, :].bitcast(F32),
                                            ALU.subtract).then_inc(gv_lo_done, 1)

            def gate_value(g, s):
                k, b = hidden_rows(s), bank(g, s)
                f = (s - ES) // 2
                dve.wait_ge(gate_done, g.n * FC + f + 1)
                dve.wait_ge(hid_mm, g.n * SLOTS + s + 1)
                nc.vector.tensor_tensor(gv[f % 2][0:k, :], hid[b][0:k, :], gate[0:k, :], ALU.mult).then_inc(gv_done, 1)

            def scale_expert(g, e):
                if e == 0:
                    passed(dve, moe_silu_done, g.n)
                elif e >= 3:
                    dve.wait_ge(moe_added, g.n * (E - 1) + e - 2)
                dve.wait_ge(s_b_done[e % 4], g.n * (E // 4 * 16) + (e // 4 + 1) * 16)
                dve.wait_ge(y_mm, g.n * YS + e + 1)
                nc.vector.scalar_tensor_tensor((ys[e % 2] if e else moe)[:], y[y_bank(g, e)][:], vecT[:, e:e + 1],
                                               s_b[e % 4][:], ALU.add, ALU.mult).then_inc(y_scaled, 1)

            def second_residual(g):
                dve.wait_ge(y_mm, g.n * YS + YS)
                nc.vector.tensor_tensor(s_sum[:], y[y_bank(g, E)][:], x1[g.parity][:], ALU.add).then_inc(s_sum_done, 1)

            def gated(g):
                dve.wait_ge(moe_silu_done, g.n + 1)
                dve.wait_ge(s_sum_done, g.n + 1)
                nc.vector.tensor_tensor(sg[:], s_sum[:], moe_silu[:], ALU.mult).then_inc(sg_done, 1)

            def result(g):
                dve.wait_ge(sg_t, g.n + 1)
                xg = x_all[:, bass.ds(g.n, 1), :, :].rearrange("p o j d -> p (o j d)")
                nc.vector.tensor_tensor(xg, m1[:], xg, ALU.add).then_inc(out_done, 1)

            g0 = Group(0, 0, 0)
            statistics(g0)
            mean_square(g0)
            dve.wait_ge(lam_done, 17)
            nc.vector.tensor_scalar(lam[:], lam_tanh[:], 0.5, 0.5, ALU.mult, ALU.add).then_inc(lam_done, 1)
            dve.wait_ge(lam_done, 18)
            nc.vector.tensor_scalar(lam_b[:], lam_b[:], lam[:, 0:1], None, ALU.mult).then_inc(lam_done, 1)
            dve.wait_ge(wt_t, 1)
            nc.vector.tensor_copy(vecT[:], hid[0][:, 0:E + 3]).then_inc(small_wt, 1)
            dve.wait_ge(small_wt, 1)
            dve.wait_ge(small_loaded, 16 * 8)
            nc.vector.tensor_tensor(Wg_raw[:], Wg_raw[:], Wg_row0[:], ALU.subtract)
            nc.vector.tensor_tensor(D_w[:], vecT[:, E:E + 1], vecT[:, E + 1:E + 2], ALU.mult).then_inc(small_wt, 1)
            nc.vector.tensor_scalar(BT[:, 0:NS], hid[1][:, 0:NS], vecT[:, E + 1:E + 2], None, ALU.mult)
            nc.vector.tensor_copy(CT[:], hid[2][0:NS, 0:D]).then_inc(small_wt, 1)
            xn_low(g0)
            dve.wait_ge(small_hi, 1)
            nc.vector.tensor_tensor(Wg_parts[:, 1, :], Wg_raw[:], Wg_parts[:, 0, :].bitcast(F32), ALU.subtract)
            nc.vector.tensor_tensor(BT_lo[:], BT[:], BT_hi[:].bitcast(F32), ALU.subtract)
            nc.vector.tensor_tensor(C_stack[2 * NS:3 * NS, :], CT[:], C_stack[0:NS, :].bitcast(F32),
                                    ALU.subtract).then_inc(small_lo, 1)
            u_low(g0)
            skip_sum(g0)
            dve.wait_ge(W1_loaded, 32)
            nc.vector.tensor_tensor(W1_raw[:], W1_raw[:], W1_row0[:], ALU.subtract).then_inc(W1_shift, 1)
            route_sum(g0)
            scan(g0)
            route_top(g0)
            route_scores(g0)
            hs_low(g0)
            dve.wait_ge(W1_hi_done, 1)
            nc.vector.tensor_tensor(W1_lo[:], W1_raw[:], W1_hi[:].bitcast(F32), ALU.subtract).then_inc(W1_lo_done, 1)
            first_residual(g0)
            z_mean_square(g0)
            low_part(g0, 0)
            low_part(g0, 1)
            dve.wait_ge(W2_hi_done, 1)
            nc.vector.tensor_tensor(W2_lo[:], W2_raw[:], W2_hi[:].bitcast(F32), ALU.subtract).then_inc(W2_lo_done, 1)
            dve.wait_ge(wt_t, 2)
            for i in range(2):
                last = nc.vector.tensor_scalar(w13T[i][:], (y[0], y[1])[i][:, 0:FF], vecT[:, E + 2:E + 3], None, ALU.mult)
            last.then_inc(ffn_wt, 1)
            for c in range(FC):
                k = hidden_rows(ES + 2 * c)
                last = nc.vector.tensor_copy(w2T[0:k, c, :], hid[3][0:k, c * D:c * D + D])
            last.then_inc(ffn_wt, 2)
            dve.wait_ge(ffn_hi, 1)
            for i in range(2):
                nc.vector.tensor_tensor(w13T_lo[i][:], w13T[i][:], w13T_hi[i][:].bitcast(F32), ALU.subtract)
            for c in range(FC):
                k = hidden_rows(ES + 2 * c)
                last = nc.vector.tensor_tensor(w2T_lo[0:k, c, :], w2T[0:k, c, :], w2T_hi[0:k, c, :].bitcast(F32),
                                               ALU.subtract)
            last.then_inc(ffn_lo, 1)

            def slot(g, c, last):
                n = after(g) if c >= FIRST else g
                nxt = ahead(g, c, 1, last)
                if nxt and nxt[1] >= ES:
                    low_part(*nxt)
                nxt = ahead(g, c, 2, last)
                if nxt and nxt[1] < ES:
                    low_part(*nxt)
                elif nxt and nxt[1] % 2:
                    gate_value(*nxt)
                if c % 2 == 0 and 2 <= c < ES + 2:
                    scale_expert(g, (c - 2) // 2)
                if c >= FIRST and not last:
                    if c == 4:
                        statistics(n)
                    if c == 6:
                        mean_square(n)
                    if c == 11:
                        xn_low(n)
                    if c == 12:
                        u_low(n)
                        skip_sum(n)
                    if c == 15:
                        route_sum(n)
                        scan(n)
                        route_top(n)
                    if c == 17:
                        route_scores(n)
                    if c == 18:
                        hs_low(n)
                    if c == 21:
                        first_residual(n)

            for c in range(FIRST):
                slot(g0, c, False)

            def step(g, last):
                for gg, c in time_slots(g, last):
                    slot(gg, c, last)
                    if c == 0:
                        second_residual(g)
                    if c == 1:
                        gated(g)
                    if c == 2:
                        z_mean_square(gg)
                    if c == 3:
                        result(g)
                if last:
                    second_residual(g)
                    gated(g)
                    result(g)

            iterations(dve, step)

        @block.tensor
        def _(pe):
            def three(out_ap, w_hi, w_lo, v_hi, v_lo, start=True, stop=True):
                pe.matmul(out_ap, w_hi, v_hi, start=start, stop=False)
                pe.matmul(out_ap, w_hi, v_lo, start=False, stop=False)
                return pe.matmul(out_ap, w_lo, v_hi, start=False, stop=stop)

            def xn_transpose(g):
                pe.wait_ge(xn_tok_done, g.n + 1)
                for j in range(TT):
                    last = pe.transpose(m0[:, j * P:(j + 1) * P], xn_tok[:, j, :], ident[:])
                last.then_inc(xn_t, 1)

            def u_transpose(g):
                pe.wait_ge(u_tok_done, g.n + 1)
                for j in range(TT):
                    last = pe.transpose(m1[:, j * P:(j + 1) * P], u_tok[:, j, :], ident[:])
                last.then_inc(u_t, 1)

            def router(g):
                pe.wait_ge(base_done, g.n + 1)
                pe.wait_ge(bias_row, g.n + 1)
                for j in range(TT):
                    cols = slice(j * P, (j + 1) * P)
                    products = m0[:, 2 * j * E:2 * (j + 1) * E]
                    parts = Wg_parts[:].rearrange("p i e -> p (i e)")
                    pe.matmul(products, xn_hi[g.parity][:, cols], parts, start=True, stop=False)
                    last = pe.matmul(products, xn_lo[g.parity][:, cols], parts, start=False, stop=True)
                last.then_inc(logits_mm, 1)

            def state_input(g):
                pe.wait_ge(u_lo_done, g.n + 1)
                three(m1[:], BT_hi[:], BT_lo[:], u_hi[:], u_lo[:]).then_inc(bu_mm, 1)

            def score_transpose(g):
                pe.wait_ge(s_tok_done, g.n + 1)
                for j in range(TT):
                    last = pe.transpose(m0[0:E, j * P:(j + 1) * P], s_tok[:, j, :], ident[:])
                last.then_inc(s_t, 1)

            def state_output(g):
                pe.wait_ge(s_row_done, g.n + 1)
                pe.wait_ge(hs_lo_done, g.n + 1)
                pe.matmul(m0[:], C_stack[:], hs_stack[:], start=True, stop=True).then_inc(c_mm, 1)

            def z_sums(g):
                pe.wait_ge(sq_done, g.n + 1)
                for j in range(TT):
                    last = pe.matmul(m0[:, j:j + 1], x1_sq[:, j * P:(j + 1) * P], ones[:, 0:1], start=True, stop=True)
                last.then_inc(ms_mm, 1)

            def r_transpose(g):
                pe.wait_ge(z_r_done, g.n + 1)
                for j in range(TT):
                    last = pe.transpose(m0[0:1, j * P:(j + 1) * P], z_r[:, j:j + 1], ident[:])
                last.then_inc(r_t, 1)

            def result_transpose(g):
                pe.wait_ge(sg_done, g.n + 1)
                for j in range(TT):
                    last = pe.transpose(m1[:, j * P:(j + 1) * P], sg[:, j * P:(j + 1) * P], ident[:])
                last.then_inc(sg_t, 1)

            def first_product(g, s):
                k, b = hidden_rows(s), bank(g, s)
                if s < ES:
                    if s == 0:
                        pe.wait_ge(bias_row, g.n + 1)
                    if s in (0, 2):
                        passed(pe, gate_done, g.n * FC - 1 + s // 2)
                    e, c = s // HC, s % HC
                    cols = slice(c * P, (c + 1) * P)
                    last = three(hid[b][:], W1_hi[:, e, cols], W1_lo[:, e, cols], xn_hi[g.parity][:], xn_lo[g.parity][:])
                else:
                    f, i = (s - ES) // 2, (s - ES) % 2
                    if s == ES:
                        pe.wait_ge(z_lo_done, g.n + 1)
                    if s == ES + 4:
                        pe.wait_ge(gate_done, g.n * FC + 1)
                    cols = slice(f * P, f * P + k)
                    last = three(hid[b][0:k, :], w13T_hi[i][:, cols], w13T_lo[i][:, cols], z_hi[:], z_lo[:])
                last.then_inc(hid_mm, 1)

            def second_product(g, s):
                k, b = hidden_rows(s), bank(g, s)
                if s < ES:
                    e, c = s // HC, s % HC
                    if c == 0:
                        if e == 1:
                            passed(pe, s_sum_done, g.n)
                        else:
                            passed(pe, y_scaled, g.n * E + (e - 1 if e else 0))
                    pe.wait_ge(h_lo_done, g.n * ES + s + 1)
                    last = three(y[y_bank(g, e)][:], W2_hi[:, e, c, :], W2_lo[:, e, c, :], h_hi[b][:], h_lo[b][:],
                                 start=(c == 0), stop=(c == HC - 1))
                    if c == HC - 1:
                        last.then_inc(y_mm, 1)
                elif s % 2:
                    f = (s - ES) // 2
                    if f == 0:
                        pe.wait_ge(y_scaled, g.n * E + E - 1)
                    pe.wait_ge(gv_lo_done, g.n * FC + f + 1)
                    last = three(y[y_bank(g, E)][:], w2T_hi[0:k, f, :], w2T_lo[0:k, f, :], h_hi[b][0:k, :], h_lo[b][0:k, :],
                                 start=(f == 0), stop=(f == FC - 1))
                    if f == FC - 1:
                        last.then_inc(y_mm, 1)

            g0 = Group(0, 0, 0)
            pe.wait_ge(ident_made, 2)
            pe.wait_ge(small_loaded, 16 * 8)
            pe.transpose(hid[0][:, 0:E + 3], vec_rows[:], ident[0:E + 3, 0:E + 3])
            pe.transpose(hid[1][:, 0:NS], Bw_raw[:], ident[0:NS, 0:NS])
            pe.transpose(hid[2][0:NS, 0:D], Cw_raw[:], ident[:]).then_inc(wt_t, 1)
            xn_transpose(g0)
            u_transpose(g0)
            pe.wait_ge(ffn_loaded, 16 * 5)
            for i, raw in enumerate((w1_raw, w3_raw)):
                for c in range(FC):
                    k = hidden_rows(ES + 2 * c)
                    pe.transpose(y[i][:, c * P:c * P + k], raw[0:k, c, :], ident[0:k, 0:k])
            for c in range(FC):
                k = hidden_rows(ES + 2 * c)
                last = pe.transpose(hid[3][0:k, c * D:c * D + D], w2_raw[:, c * P:c * P + k], ident[:])
            last.then_inc(wt_t, 1)
            pe.wait_ge(small_lo, 1)
            router(g0)
            state_input(g0)
            score_transpose(g0)
            state_output(g0)
            z_sums(g0)
            pe.wait_ge(W1_lo_done, 1)
            first_product(g0, 0)
            first_product(g0, 1)
            first_product(g0, 2)
            pe.wait_ge(W2_lo_done, 1)
            pe.wait_ge(ffn_lo, 1)

            def slot(g, c, last):
                n = after(g) if c >= FIRST else g
                nxt = ahead(g, c, AHEAD, last)
                if nxt:
                    first_product(*nxt)
                second_product(g, c)
                if c == 4:
                    r_transpose(g)
                if c >= FIRST and not last:
                    if c == 9:
                        xn_transpose(n)
                    if c == 10:
                        u_transpose(n)
                    if c == 13:
                        state_input(n)
                    if c == 14:
                        router(n)
                    if c == 18:
                        score_transpose(n)
                    if c == 20:
                        state_output(n)

            for c in range(FIRST):
                slot(g0, c, False)

            def step(g, last):
                for gg, c in time_slots(g, last):
                    slot(gg, c, last)
                    if c == 1:
                        z_sums(gg)
                    if c == 2:
                        result_transpose(g)
                if last:
                    result_transpose(g)

            iterations(pe, step)


_INS = ['L0_attn_x', 'L0_attn_log_lambda', 'L0_attn_B_w', 'L0_attn_C_w', 'L0_attn_D_skip', 'L0_attn_ssm_norm_w',
        'L0_attn_ffn_norm_w', 'L0_attn_w1', 'L0_attn_w2', 'L0_attn_w3', 'L0_ffn_Wg', 'L0_ffn_W1', 'L0_ffn_b1',
        'L0_ffn_W2', 'L0_ffn_b2']
_OUTS = [((B, T, D), 'float32')]


def kernel(**inputs):
    import numpy as _np
    import concourse.bacc as _bacc
    from concourse import mybir as _mybir
    from concourse.bass_utils import run_bass_kernel_spmd as _run

    nc = _bacc.Bacc("TRN2", target_bir_lowering=False, num_devices=1)
    arrays, args = {}, []
    for name in _INS:
        a = _np.ascontiguousarray(inputs[name])
        arrays[f"in_{name}_dram"] = a
        args.append(nc.dram_tensor(f"in_{name}_dram", a.shape, _mybir.dt.from_np(a.dtype), kind="ExternalInput").ap())
    for i, (shape, dtype) in enumerate(_OUTS):
        dt = _mybir.dt.from_np(_np.dtype(dtype))
        args.append(nc.dram_tensor(f"out_{i}_dram", shape, dt, kind="ExternalOutput").ap())
    build(nc, *args)
    r = _run(nc, [arrays], core_ids=[0])
    got = tuple(r.results[0][f"out_{i}_dram"] for i in range(len(_OUTS)))
    return got[0]
```

```python
from collections import namedtuple
from contextlib import ExitStack

import concourse.bass as bass
from concourse import mybir

P = 128
D = 128
B = 16
T = 512
TT = T // P
NS = 32
FF = 344
FC = (FF + P - 1) // P
E = 8
H = 256
HC = H // P
ES = E * HC
SLOTS = ES + 2 * FC
YS = E + 1
PART = 2
PARTS = E // PART
AHEAD = 3
FIRST = 6
STEPS = 6
LN_EPS = 1e-5
RMS_EPS = 1e-6

F32 = mybir.dt.float32
F32R = mybir.dt.float32r
U32 = mybir.dt.uint32
ALU = mybir.AluOpType
ACT = mybir.ActivationFunctionType

Group = namedtuple("Group", "n half parity")


def after(g):
    return Group(g.n + 1, g.half + g.parity, 1 - g.parity)


def hidden_rows(s):
    return P if s < ES else min(P, FF - (s - ES) // 2 * P)


def build(nc, x, log_lambda, B_w, C_w, D_skip, ssm_norm_w, ffn_norm_w, w1, w2, w3, Wg, W1, b1, W2, b2, out):
    x_v = x.rearrange("b (j p) d -> b p j d", p=P)
    out_v = out.rearrange("b (j p) d -> b p j d", p=P)

    with ExitStack() as ctx:
        def sb(name, shape, dt=F32):
            return ctx.enter_context(nc.sbuf_tensor(name, shape, dt))

        def psum(name, shape):
            return ctx.enter_context(nc.psum_tensor(name, shape, F32))

        def sem(name):
            return ctx.enter_context(nc.semaphore(name))

        W1_raw = sb("W1_raw", [P, E, H])
        W1_row0 = sb("W1_row0", [P, E, H])
        W2_raw = sb("W2_raw", [P, E, HC, D])
        Wg_raw = sb("Wg_raw", [P, E])
        w1_raw = sb("w1_raw", [P, FC, D])
        w3_raw = sb("w3_raw", [P, FC, D])
        w2_raw = sb("w2_raw", [P, FF])
        Bw_raw = sb("Bw_raw", [NS, D])
        Cw_raw = sb("Cw_raw", [D, NS])
        vec_rows = sb("vec_rows", [E + 3, D])
        log_lam = sb("log_lam", [NS, 1])
        W1_hi, W1_lo = sb("W1_hi", [P, E, H], F32R), sb("W1_lo", [P, E, H], F32R)
        W2_hi, W2_lo = sb("W2_hi", [P, E, HC, D], F32R), sb("W2_lo", [P, E, HC, D], F32R)
        w1T, w3T = sb("w1T", [P, FF]), sb("w3T", [P, FF])
        w13T = [w1T, w3T]
        w13T_hi = [sb("w1T_hi", [P, FF], F32R), sb("w3T_hi", [P, FF], F32R)]
        w13T_lo = [sb("w1T_lo", [P, FF], F32R), sb("w3T_lo", [P, FF], F32R)]
        w2T = sb("w2T", [P, FC, D])
        w2T_hi, w2T_lo = sb("w2T_hi", [P, FC, D], F32R), sb("w2T_lo", [P, FC, D], F32R)
        BT = sb("BT", [P, P])
        BT_hi, BT_lo = sb("BT_hi", [P, P], F32R), sb("BT_lo", [P, P], F32R)
        CT = sb("CT", [NS, D])
        C_stack = sb("C_stack", [3 * NS, D], F32R)
        vecT = sb("vecT", [P, E + 3])
        D_w = sb("D_w", [P, 1])
        lam_tanh, lam = sb("lam_tanh", [NS, 1]), sb("lam", [NS, 1])
        lam_b = sb("lam_b", [NS, T])
        ident = sb("ident", [P, P])
        ones = sb("ones", [P, 1])
        warm = sb("warm", [P, 1])
        minus_half = sb("minus_half", [P, TT])
        expert_no = sb("expert_no", [P, TT, E])
        x_all = sb("x_all", [P, B, TT, D])
        bn = sb("bn", [P, TT, 6])
        shift = sb("shift", [P, TT])
        mean_sum, mean_gap, square_sum = sb("mean_sum", [P, TT]), sb("mean_gap", [P, TT]), sb("square_sum", [P, TT])
        mean, gap_square, var = sb("mean", [P, TT]), sb("gap_square", [P, TT]), sb("var", [P, TT])
        var_eps, rstd = sb("var_eps", [P, TT]), sb("rstd", [P, TT])
        rstd2, msq, msq_eps, rrms = sb("rstd2", [P, TT]), sb("msq", [P, TT]), sb("msq_eps", [P, TT]), sb("rrms", [P, TT])
        xn_tok = sb("xn_tok", [P, TT, D])
        xn_hi = [sb(f"xn_hi{i}", [P, T], F32R) for i in range(2)]
        xn_lo = [sb(f"xn_lo{i}", [P, T], F32R) for i in range(2)]
        rrms_rows, rrms_b = sb("rrms_rows", [TT, P]), sb("rrms_b", [P, T])
        base = sb("base", [P, T])
        skip_w = sb("skip_w", [P, T])
        logits = sb("logits", [P, TT, E])
        top, top_i = sb("top", [P, TT, 8]), sb("top_i", [P, TT, 8], U32)
        gap, gap_tanh = sb("gap", [P, TT]), sb("gap_tanh", [P, TT])
        score = [sb(f"score{k}", [P, TT]) for k in range(2)]
        chosen = [sb(f"chosen{k}", [P, TT, E]) for k in range(2)]
        part = [sb(f"part{k}", [P, TT, E]) for k in range(2)]
        s_tok = sb("s_tok", [P, TT, E])
        s_row = sb("s_row", [E, T])
        s_b = [sb(f"s_b{i}", [P, T]) for i in range(4)]
        bu, hs = sb("bu", [NS, T]), sb("hs", [NS, T])
        hs_stack = sb("hs_stack", [3 * NS, T], F32R)
        x1 = [sb(f"x1_{i}", [P, T]) for i in range(2)]
        x1_sq = sb("x1_sq", [P, T])
        z_msq, z_r = sb("z_msq", [P, TT]), sb("z_r", [P, TT])
        r_rows, r_b = sb("r_rows", [TT, P]), sb("r_b", [P, T])
        z = sb("z", [P, T])
        z_hi, z_lo = sb("z_hi", [P, T], F32R), sb("z_lo", [P, T], F32R)
        h_hi = [sb(f"h_hi{i}", [P, T], F32R) for i in range(4)]
        h_lo = [sb(f"h_lo{i}", [P, T], F32R) for i in range(4)]
        gate, gv = sb("gate", [P, T]), [sb(f"gv{i}", [P, T]) for i in range(2)]
        ys = [sb(f"ys{i}", [P, T]) for i in range(2)]
        moe, moe_silu = sb("moe", [P, T]), sb("moe_silu", [P, T])
        s_sum, sg = sb("s_sum", [P, T]), sb("sg", [P, T])

        hid = [psum(f"hid{i}", [P, T]) for i in range(4)]
        y = [psum(f"y{i}", [P, T]) for i in range(2)]
        m0, m1 = psum("m0", [P, T]), psum("m1", [P, T])

        x_loaded = [sem("x_even_loaded"), sem("x_odd_loaded")]
        small_loaded, ffn_loaded = sem("small_loaded"), sem("ffn_loaded")
        W1_loaded, W1_rest_loaded = sem("W1_loaded"), sem("W1_rest_loaded")
        W2_loaded, W2_rest_loaded = sem("W2_loaded"), sem("W2_rest_loaded")
        stored = sem("stored")
        pool_consts, dve_consts, ident_made = sem("pool_consts"), sem("dve_consts"), sem("ident_made")
        lam_done, wt_t = sem("lam_done"), sem("wt_t")
        small_wt, small_hi, small_lo = sem("small_wt"), sem("small_hi"), sem("small_lo")
        ffn_wt, ffn_hi, ffn_lo = sem("ffn_wt"), sem("ffn_hi"), sem("ffn_lo")
        W1_shifted, W1_hi_done, W1_lo_done = sem("W1_shifted"), sem("W1_hi_done"), sem("W1_lo_done")
        W2_hi_done, W2_lo_done = sem("W2_hi_done"), sem("W2_lo_done")
        stats_step = sem("stats_step")
        var_done, shift_done, msq_done = sem("var_done"), sem("shift_done"), sem("msq_done")
        rstd_done, rrms_done = sem("rstd_done"), sem("rrms_done")
        xn_tok_done = sem("xn_tok_done")
        xn_t, rrms_t = sem("xn_t"), sem("rrms_t")
        xn_copied, xn_hi_done = sem("xn_copied"), sem("xn_hi_done")
        rrms_rows_done, rrms_b_done, skip_w_done = sem("rrms_rows_done"), sem("rrms_b_done"), sem("skip_w_done")
        xn_lo_done, base_done = sem("xn_lo_done"), sem("base_done")
        bias_row = sem("bias_row")
        logits_mm, bu_mm, s_t = sem("logits_mm"), sem("bu_mm"), sem("s_t")
        route_step, gap_done, scored, s_tok_done = sem("route_step"), sem("gap_done"), sem("scored"), sem("s_tok_done")
        tanh_done, s_row_done = sem("tanh_done"), sem("s_row_done")
        s_b_done = [sem(f"s_b{i}_done") for i in range(4)]
        bu_done, hs_done, hs_lo_done, hs_hi_done = sem("bu_done"), sem("hs_done"), sem("hs_lo_done"), sem("hs_hi_done")
        c_mm, x1_done, sq_done, ms_mm = sem("c_mm"), sem("x1_done"), sem("sq_done"), sem("ms_mm")
        z_msq_done, z_r_done, r_t, r_rows_done = sem("z_msq_done"), sem("z_r_done"), sem("r_t"), sem("r_rows_done")
        r_b_done, z_done, z_hi_done, z_lo_done = sem("r_b_done"), sem("z_done"), sem("z_hi_done"), sem("z_lo_done")
        hid_mm, y_mm = sem("hid_mm"), sem("y_mm")
        h_hi_done, h_lo_done = sem("h_hi_done"), sem("h_lo_done")
        gate_done, gv_done, gv_hi_done, gv_lo_done = sem("gate_done"), sem("gv_done"), sem("gv_hi_done"), sem("gv_lo_done")
        y_scaled, moe_added = sem("y_scaled"), sem("moe_added")
        moe_silu_done, s_sum_done, sg_done, sg_t, out_done = sem("moe_silu_done"), sem("s_sum_done"), sem("sg_done"), sem("sg_t"), sem("out_done")

        def bank(g, s):
            return (g.parity * SLOTS + s) % 4

        def y_bank(g, k):
            return (g.parity * YS + k) % 2

        def passed(eng, semaphore, value):
            if not isinstance(value, int) or value > 0:
                eng.wait_ge(semaphore, value)


        def has_next(g):
            return not isinstance(g.n, int) or g.n < B - 1

        def iterations(eng, slot):
            def group(g):
                for c in range(FIRST, SLOTS):
                    slot(g, c)
                if has_next(g):
                    for c in range(FIRST):
                        slot(after(g), c)

            for c in range(FIRST):
                slot(Group(0, 0, 0), c)
            with eng.Fori(0, B // 2 - 1) as pair:
                group(Group(pair * 2, pair, 0))
                group(Group(pair * 2 + 1, pair, 1))
            group(Group(B - 2, B // 2 - 1, 0))
            group(Group(B - 1, B // 2 - 1, 1))

        def before(g):
            if isinstance(g.n, int) and g.n == 0:
                return None
            return Group(g.n - 1, g.half + g.parity - 1, 1 - g.parity)

        def ahead(g, c, by):
            if c + by < SLOTS:
                return g, c + by
            return (after(g), c + by - SLOTS) if has_next(g) else None

        def is_first(g):
            return isinstance(g.n, int) and g.n == 0

        block = ctx.enter_context(nc.Block())

        @block.sync
        def _(sp):
            def load(g):
                passed(sp, x_loaded[g.parity], g.half * 16)
                sp.dma_start(x_all[:, bass.ds(g.n, 1), :, :].rearrange("p o j d -> p (o j) d"),
                             x_v[bass.ds(g.n, 1)].rearrange("o p j d -> p (o j) d")).then_inc(x_loaded[g.parity], 16)

            def broadcast_score(g, e):
                passed(sp, y_scaled, g.n * E + e - 3)
                if e == 0:
                    sp.wait_ge(s_row_done, g.n + 1)
                sp.dma_start(s_b[e % 4][:], s_row[e:e + 1, :].unsqueeze(1).to_broadcast([1, P, T])).then_inc(s_b_done[e % 4], 16)

            def broadcast_rows(rows, to, done):
                for j in range(TT):
                    sp.dma_start(to[:, j * P:(j + 1) * P],
                                 rows[j:j + 1, :].unsqueeze(1).to_broadcast([1, P, P])).then_inc(done, 16)

            def broadcast_rrms(g):
                sp.wait_ge(rrms_rows_done, g.n + 1)
                broadcast_rows(rrms_rows, rrms_b, rrms_b_done)

            def broadcast_r(g):
                sp.wait_ge(r_rows_done, g.n + 1)
                broadcast_rows(r_rows, r_b, r_b_done)

            def store(g):
                sp.wait_ge(out_done, g.n + 1)
                sp.dma_start(out_v[bass.ds(g.n, 1)].rearrange("o p j d -> p (o j) d"),
                             x_all[:, bass.ds(g.n, 1), :, :].rearrange("p o j d -> p (o j) d")).then_inc(stored, 16)

            g0 = Group(0, 0, 0)
            def load_W1(experts, done):
                n = experts.stop - experts.start
                sp.dma_start(W1_raw[1:P, experts], W1[experts, 1:P, :].rearrange("e d h -> d e h")).then_inc(done, 16)
                sp.dma_start(W1_row0[1:P, experts], W1[experts, 0:1, :].rearrange("e d h -> d e h")
                             .to_broadcast([P - 1, n, H])).then_inc(done, 16)

            def load_W2(experts, done):
                sp.dma_start(W2_raw[:, experts], W2[experts].rearrange("e (c p) d -> p e c d", p=P)).then_inc(done, 16)

            load(g0)
            load_W1(slice(0, PART), W1_loaded)
            sp.dma_start(W1_raw[0:1], b1.rearrange("(o e) h -> o e h", o=1)).then_inc(W1_loaded, 16)
            load_W2(slice(0, PART), W2_loaded)
            load_W1(slice(PART, E), W1_rest_loaded)
            sp.dma_start(log_lam[:], log_lambda.rearrange("(n o) -> n o", o=1)).then_inc(lam_done, 16)
            load_W2(slice(PART, E), W2_rest_loaded)
            full = FF // P * P
            for w, raw in ((w1, w1_raw), (w3, w3_raw)):
                sp.dma_start(raw[:, 0:FF // P, :], w[0:full, :].rearrange("(c p) d -> p c d", p=P)).then_inc(ffn_loaded, 16)
                sp.dma_start(raw[0:FF - full, FC - 1, :], w[full:FF, :]).then_inc(ffn_loaded, 16)
            sp.dma_start(w2_raw[:], w2).then_inc(ffn_loaded, 16)
            load(after(g0))
            broadcast_rrms(g0)

            def slot(g, c):
                if c == 1:
                    for e in range(4):
                        broadcast_score(g, e)
                if c in (2, 6, 8, 10):
                    broadcast_score(g, {2: 4, 6: 5, 8: 6, 10: 7}[c])
                if c == 4:
                    broadcast_r(g)
                if c == 5 and before(g):
                    store(before(g))
                if has_next(g):
                    if c == FIRST and not isinstance(g.n, int):
                        load(after(after(g)))
                    if c == 11:
                        broadcast_rrms(after(g))

            iterations(sp, slot)
            store(Group(B - 1, B // 2 - 1, 1))
            sp.wait_ge(stored, B * 16)

        @block.gpsimd
        def _(pool):
            nc.gpsimd.memset(ident[:], 0.0).then_inc(ident_made, 1)
            pool.wait_ge(ident_made, 1)
            nc.gpsimd.affine_select(out=ident[:], in_=ident[:], compare_op=ALU.not_equal, fill=1.0, base=0,
                                    pattern=[[-1, P]], channel_multiplier=1).then_inc(ident_made, 1)
            nc.gpsimd.memset(minus_half[:], -0.5)
            nc.gpsimd.memset(ones[:], 1.0).then_inc(pool_consts, 1)
            pool.wait_ge(pool_consts, 1)

            def rstd_pow(g):
                pool.wait_ge(var_done, g.n + 1)
                nc.gpsimd.tensor_tensor(rstd[:], var_eps[:], minus_half[:], ALU.pow).then_inc(rstd_done, 1)

            def rrms_pow(g):
                pool.wait_ge(msq_done, g.n + 1)
                nc.gpsimd.tensor_tensor(rrms[:], msq_eps[:], minus_half[:], ALU.pow).then_inc(rrms_done, 1)

            def xn_low(g):
                pool.wait_ge(xn_hi_done, g.n + 1)
                nc.gpsimd.tensor_tensor(xn_lo[g.parity][:], base[:], xn_hi[g.parity][:].bitcast(F32),
                                        ALU.subtract).then_inc(xn_lo_done, 1)

            def bias_rows(g):
                pool.wait_ge(pool_consts, 1)
                pool.wait_ge(bu_mm, g.n + 1)
                nc.gpsimd.memset(xn_hi[g.parity][0:1, :].bitcast(F32), 1.0)
                nc.gpsimd.memset(xn_lo[g.parity][0:1, :].bitcast(F32), 0.0).then_inc(bias_row, 1)

            def skip_sum(g):
                pool.wait_ge(skip_w_done, g.n + 1)
                pool.wait_ge(logits_mm, g.n + 1)
                nc.gpsimd.tensor_tensor(base[:], base[:], skip_w[:], ALU.mult).then_inc(base_done, 1)

            def add_expert(g, e):
                if e >= 2:
                    pool.wait_ge(moe_added, g.n * (E - 1) + e - 1)
                pool.wait_ge(y_scaled, g.n * E + e + 1)
                nc.gpsimd.tensor_tensor(moe[:], moe[:], ys[e % 2][:], ALU.add).then_inc(moe_added, 1)

            def gated(g):
                pool.wait_ge(s_sum_done, g.n + 1)
                pool.wait_ge(moe_silu_done, g.n + 1)
                nc.gpsimd.tensor_tensor(sg[:], s_sum[:], moe_silu[:], ALU.mult).then_inc(sg_done, 1)

            def z_pow(g):
                pool.wait_ge(z_msq_done, g.n + 1)
                nc.gpsimd.tensor_tensor(z_r[:], z_msq[:], minus_half[:], ALU.pow).then_inc(z_r_done, 1)

            def z_scale(g):
                pool.wait_ge(r_b_done, g.n * (TT * 16) + TT * 16)
                nc.gpsimd.tensor_tensor(z[:], x1[g.parity][:], r_b[:], ALU.mult).then_inc(z_done, 1)

            def z_low(g):
                pool.wait_ge(z_hi_done, g.n + 1)
                nc.gpsimd.tensor_tensor(z_lo[:], z[:], z_hi[:].bitcast(F32), ALU.subtract).then_inc(z_lo_done, 1)

            def W2_low(k):
                experts = slice(k * PART, (k + 1) * PART)
                pool.wait_ge(W2_hi_done, k + 1)
                nc.gpsimd.tensor_tensor(W2_lo[:, experts], W2_raw[:, experts], W2_hi[:, experts].bitcast(F32),
                                        ALU.subtract).then_inc(W2_lo_done, 1)

            def ffn_low():
                pool.wait_ge(ffn_hi, 1)
                for i in range(2):
                    nc.gpsimd.tensor_tensor(w13T_lo[i][:], w13T[i][:], w13T_hi[i][:].bitcast(F32), ALU.subtract)
                for c in range(FC):
                    k = hidden_rows(ES + 2 * c)
                    last = nc.gpsimd.tensor_tensor(w2T_lo[0:k, c, :], w2T[0:k, c, :], w2T_hi[0:k, c, :].bitcast(F32),
                                                   ALU.subtract)
                last.then_inc(ffn_lo, 1)

            g0 = Group(0, 0, 0)
            rstd_pow(g0)
            rrms_pow(g0)
            xn_low(g0)
            bias_rows(g0)
            W2_low(0)
            skip_sum(g0)

            def slot(g, c):
                n = after(g) if has_next(g) else None
                if is_first(g) and c < PARTS - 1:
                    W2_low(c + 1)
                if c == 3:
                    z_pow(g)
                if c == 4 and n:
                    rstd_pow(n)
                if c == 5:
                    add_expert(g, 1)
                    if is_first(g):
                        ffn_low()
                if c == 10:
                    add_expert(g, 2)
                if c == 11 and n:
                    rrms_pow(n)
                if c == 12:
                    z_scale(g)
                    add_expert(g, 3)
                    z_low(g)
                    add_expert(g, 4)
                if c == 14 and n:
                    xn_low(n)
                if c == 14:
                    add_expert(g, 5)
                if c == 15 and n:
                    bias_rows(n)
                if c == 15:
                    add_expert(g, 6)
                if c == 18:
                    add_expert(g, 7)
                    if n:
                        skip_sum(n)
                if c == 20:
                    gated(g)

            iterations(pool, slot)

        @block.scalar
        def _(act):
            act.dma_start(Bw_raw[:], B_w).then_inc(small_loaded, 16)
            act.dma_start(vec_rows[0:E, :], b2).then_inc(small_loaded, 16)
            for k, v in enumerate((D_skip, ssm_norm_w, ffn_norm_w)):
                act.dma_start(vec_rows[E + k:E + k + 1, :], v.rearrange("(o d) -> o d", o=1)).then_inc(small_loaded, 16)
            act.dma_start(Cw_raw[:], C_w).then_inc(small_loaded, 16)
            act.dma_start(Wg_raw[:], Wg).then_inc(small_loaded, 16)

            def xn_tokens(g, first):
                if first == 0:
                    act.wait_ge(pool_consts, 1)
                    act.wait_ge(shift_done, g.n + 1)
                for j in range(first, first + TT // 2):
                    last = nc.scalar.activation(
                        xn_tok[:, j, :], x_all[:, bass.ds(g.n, 1), j, :].rearrange("p o d -> p (o d)"),
                        ACT.Identity, bias=shift[:, j:j + 1], scale=rstd[:, j:j + 1])
                if first:
                    last.then_inc(xn_tok_done, 1)

            def xn_copy(g):
                act.wait_ge(xn_t, g.n + 1)
                nc.scalar.activation(base[:], m0[:], ACT.Copy).then_inc(xn_copied, 1)

            def xn_high(g):
                act.wait_ge(xn_copied, g.n + 1)
                nc.scalar.activation(xn_hi[g.parity][:], base[:], ACT.Copy).then_inc(xn_hi_done, 1)

            def rrms_to_rows(g):
                act.wait_ge(rrms_t, g.n + 1)
                nc.scalar.activation(rrms_rows[:], m1[0:TT, 0:P], ACT.Copy).then_inc(rrms_rows_done, 1)

            def skip_weight(g):
                act.wait_ge(rrms_b_done, g.n * (TT * 16) + TT * 16)
                nc.scalar.activation(skip_w[:], rrms_b[:], ACT.Identity, bias=ones[:, 0:1],
                                     scale=D_w[:, 0:1]).then_inc(skip_w_done, 1)

            def gap_to_tanh(g):
                act.wait_ge(gap_done, g.n + 1)
                nc.scalar.activation(gap_tanh[:], gap[:], ACT.Tanh, scale=0.5).then_inc(tanh_done, 1)

            def hs_high(g):
                act.wait_ge(hs_done, g.n + 1)
                nc.scalar.activation(hs_stack[0:NS, :], hs[:], ACT.Copy)
                nc.scalar.activation(hs_stack[2 * NS:3 * NS, :], hs[:], ACT.Copy).then_inc(hs_hi_done, 1)

            def score_rows(g):
                for i in range(4):
                    passed(act, s_b_done[i], g.n * (E // 4 * 16))
                act.wait_ge(s_t, g.n + 1)
                nc.scalar.activation(s_row[:], m0[0:E, :], ACT.Copy).then_inc(s_row_done, 1)

            def square(g):
                act.wait_ge(x1_done, g.n + 1)
                nc.scalar.activation(x1_sq[:], x1[g.parity][:], ACT.Square).then_inc(sq_done, 1)

            def r_to_rows(g):
                act.wait_ge(r_t, g.n + 1)
                nc.scalar.activation(r_rows[:], m0[0:TT, 0:P], ACT.Copy).then_inc(r_rows_done, 1)

            def z_high(g):
                act.wait_ge(z_done, g.n + 1)
                nc.scalar.activation(z_hi[:], z[:], ACT.Copy).then_inc(z_hi_done, 1)

            def evacuate(g, s):
                k, b = hidden_rows(s), bank(g, s)
                f = (s - ES) // 2
                if s < ES:
                    act.wait_ge(hid_mm, g.n * SLOTS + s + 1)
                    nc.scalar.activation(h_hi[b][:], hid[b][:], ACT.Relu).then_inc(h_hi_done, 1)
                elif s % 2 == 0:
                    act.wait_ge(hid_mm, g.n * SLOTS + s + 1)
                    nc.scalar.activation(gate[0:k, :], hid[b][0:k, :], ACT.Silu).then_inc(gate_done, 1)
                else:
                    act.wait_ge(gv_done, g.n * FC + f + 1)
                    nc.scalar.activation(h_hi[b][0:k, :], gv[f % 2][0:k, :], ACT.Copy).then_inc(gv_hi_done, 1)

            def moe_gate(g):
                act.wait_ge(moe_added, g.n * (E - 1) + E - 1)
                nc.scalar.activation(moe_silu[:], moe[:], ACT.Silu).then_inc(moe_silu_done, 1)

            g0 = Group(0, 0, 0)
            def W1_high(k):
                experts = slice(k * PART, (k + 1) * PART)
                act.wait_ge(W1_shifted, k + 1)
                nc.scalar.activation(W1_hi[:, experts], W1_raw[:, experts], ACT.Copy).then_inc(W1_hi_done, 1)

            def W2_high(k):
                experts = slice(k * PART, (k + 1) * PART)
                act.wait_ge(W2_rest_loaded if k else W2_loaded, 16)
                nc.scalar.activation(W2_hi[:, experts], W2_raw[:, experts], ACT.Copy).then_inc(W2_hi_done, 1)

            act.wait_ge(pool_consts, 1)
            nc.scalar.activation(warm[:], ones[:], ACT.Silu)
            for first in (0, TT // 2):
                xn_tokens(g0, first)
            W1_high(0)
            xn_copy(g0)
            xn_high(g0)
            rrms_to_rows(g0)
            act.wait_ge(small_wt, 3)
            nc.scalar.activation(BT_hi[:], BT[:], ACT.Copy)
            nc.scalar.activation(C_stack[0:NS, :], CT[:], ACT.Copy)
            nc.scalar.activation(C_stack[NS:2 * NS, :], CT[:], ACT.Copy).then_inc(small_hi, 1)
            W2_high(0)
            act.wait_ge(lam_done, 16)
            nc.scalar.activation(lam_tanh[:], log_lam[:], ACT.Tanh, scale=0.5).then_inc(lam_done, 1)
            gap_to_tanh(g0)
            W1_high(1)
            evacuate(g0, 0)
            skip_weight(g0)
            evacuate(g0, 1)
            hs_high(g0)
            score_rows(g0)
            W1_high(2)

            def ffn_high():
                act.wait_ge(ffn_wt, 3)
                for i in range(2):
                    nc.scalar.activation(w13T_hi[i][:], w13T[i][:], ACT.Copy)
                for c in range(FC):
                    k = hidden_rows(ES + 2 * c)
                    last = nc.scalar.activation(w2T_hi[0:k, c, :], w2T[0:k, c, :], ACT.Copy)
                last.then_inc(ffn_hi, 1)

            def slot(g, c):
                n = after(g) if has_next(g) else None
                nxt = ahead(g, c, 2)
                if nxt and nxt[1] < ES:
                    evacuate(*nxt)
                if is_first(g) and c == 1:
                    W1_high(3)
                if is_first(g) and c in (0, 2, 3):
                    W2_high({0: 1, 2: 2, 3: 3}[c])
                if c == 1 and before(g):
                    moe_gate(before(g))
                if c == 2:
                    square(g)
                if c == 4:
                    r_to_rows(g)
                if c == 5 and is_first(g):
                    ffn_high()
                if c == 7 and n:
                    xn_tokens(n, 0)
                    xn_tokens(n, TT // 2)
                if c == 10 and n:
                    xn_copy(n)
                if c == 11:
                    z_high(g)
                    if n:
                        rrms_to_rows(n)
                if c == 12 and n:
                    gap_to_tanh(n)
                if c == 14 and n:
                    xn_high(n)
                if c == 15:
                    evacuate(g, ES)
                if c == 16:
                    evacuate(g, ES + 1)
                    evacuate(g, ES + 2)
                if c == 17:
                    if n:
                        skip_weight(n)
                    evacuate(g, ES + 3)
                    evacuate(g, ES + 4)
                if c == 19:
                    if n:
                        hs_high(n)
                    evacuate(g, ES + 5)
                if c == 20 and n:
                    score_rows(n)

            iterations(act, slot)
            moe_gate(Group(B - 1, B // 2 - 1, 1))

        @block.vector
        def _(dve):
            for e in range(E):
                nc.vector.memset(expert_no[:, :, e:e + 1], float(e))
            nc.vector.memset(BT[:], 0.0)
            nc.vector.memset(lam_b[:], 1.0)
            nc.vector.memset(W1_row0[0:1], 0.0)
            nc.vector.memset(C_stack[:].bitcast(F32), 0.0).then_inc(dve_consts, 1)
            dve.wait_ge(dve_consts, 1)

            def statistics(g):
                dve.wait_ge(dve_consts, 1)
                dve.wait_ge(x_loaded[g.parity], g.half * 16 + 16)
                for j in range(TT):
                    last = nc.vector.bn_stats(bn[:, j, :], x_all[:, bass.ds(g.n, 1), j, :].rearrange("p o d -> p (o d)"))
                last.then_inc(stats_step, 1)

            def statistics_sums(g):
                half = [bn[:, :, k] for k in range(6)]
                dve.wait_ge(stats_step, g.n * STEPS + 1)
                nc.vector.tensor_tensor(mean_sum[:], half[1], half[4], ALU.add)
                nc.vector.tensor_tensor(mean_gap[:], half[1], half[4], ALU.subtract)
                nc.vector.tensor_tensor(square_sum[:], half[2], half[5], ALU.add).then_inc(stats_step, 1)

            def statistics_mean(g):
                dve.wait_ge(stats_step, g.n * STEPS + 2)
                nc.vector.tensor_scalar(mean[:], mean_sum[:], 0.5, None, ALU.mult)
                nc.vector.scalar_tensor_tensor(gap_square[:], mean_gap[:], 0.25, mean_gap[:], ALU.mult,
                                               ALU.mult).then_inc(stats_step, 1)

            def statistics_var(g):
                dve.wait_ge(stats_step, g.n * STEPS + 3)
                nc.vector.scalar_tensor_tensor(var[:], square_sum[:], 1.0 / D, gap_square[:], ALU.mult,
                                               ALU.add).then_inc(stats_step, 1)

            def statistics_eps(g):
                dve.wait_ge(stats_step, g.n * STEPS + 4)
                nc.vector.tensor_scalar(var_eps[:], var[:], LN_EPS, None, ALU.add).then_inc(var_done, 1)

            def mean_square(g):
                dve.wait_ge(rstd_done, g.n + 1)
                nc.vector.scalar_tensor_tensor(shift[:], mean[:], -1.0, rstd[:], ALU.mult, ALU.mult).then_inc(shift_done, 1)
                nc.vector.tensor_tensor(rstd2[:], rstd[:], rstd[:], ALU.mult).then_inc(stats_step, 1)

            def mean_square_var(g):
                dve.wait_ge(stats_step, g.n * STEPS + 5)
                nc.vector.tensor_tensor(msq[:], rstd2[:], var[:], ALU.mult).then_inc(stats_step, 1)

            def mean_square_eps(g):
                dve.wait_ge(stats_step, g.n * STEPS + 6)
                nc.vector.tensor_scalar(msq_eps[:], msq[:], RMS_EPS, None, ALU.add).then_inc(msq_done, 1)

            def route_logits(g):
                dve.wait_ge(logits_mm, g.n + 1)
                nc.vector.tensor_copy(logits[:].rearrange("p j e -> p (j e)"), m0[:, 0:TT * E]).then_inc(route_step, 1)

            def scale_input(g):
                dve.wait_ge(bu_mm, g.n + 1)
                dve.wait_ge(rrms_b_done, g.n * (TT * 16) + TT * 16)
                nc.vector.tensor_tensor(bu[:], m1[0:NS, :], rrms_b[0:NS, :], ALU.mult).then_inc(bu_done, 1)

            def scan(g):
                dve.wait_ge(bu_done, g.n + 1)
                nc.vector.tensor_tensor_scan(hs[:], lam_b[:], bu[:], 0.0, ALU.mult, ALU.add).then_inc(hs_done, 1)

            def route_top(g):
                for j in range(TT):
                    last = nc.vector.max(top[:, j, :], logits[:, j, :])
                last.then_inc(route_step, 1)
                dve.wait_ge(route_step, g.n * 5 + 2)
                nc.vector.tensor_tensor(gap[:], top[:, :, 0], top[:, :, 1], ALU.subtract).then_inc(gap_done, 1)

            def route_index(g):
                for j in range(TT):
                    last = nc.vector.max_index(top_i[:, j, :], top[:, j, :], logits[:, j, :])
                last.then_inc(route_step, 1)
                dve.wait_ge(route_step, g.n * 5 + 3)
                for k in range(2):
                    last = nc.vector.tensor_tensor(chosen[k][:], top_i[:, :, k:k + 1].to_broadcast([P, TT, E]),
                                                   expert_no[:], ALU.is_equal)
                last.then_inc(route_step, 1)

            def route_scores(g):
                dve.wait_ge(tanh_done, g.n + 1)
                for k, sign in enumerate((0.5, -0.5)):
                    last = nc.vector.tensor_scalar(score[k][:], gap_tanh[:], sign, 0.5, ALU.mult, ALU.add)
                last.then_inc(scored, 1)

            def route_parts(g):
                dve.wait_ge(route_step, g.n * 5 + 4)
                dve.wait_ge(scored, g.n + 1)
                for k in range(2):
                    last = nc.vector.tensor_tensor(part[k][:], chosen[k][:],
                                                   score[k][:].unsqueeze(2).to_broadcast([P, TT, E]), ALU.mult)
                last.then_inc(route_step, 1)

            def route_table(g):
                dve.wait_ge(route_step, g.n * 5 + 5)
                nc.vector.tensor_tensor(s_tok[:], part[0][:], part[1][:], ALU.add).then_inc(s_tok_done, 1)

            def hs_low(g):
                dve.wait_ge(hs_hi_done, g.n + 1)
                nc.vector.tensor_tensor(hs_stack[NS:2 * NS, :], hs[:], hs_stack[0:NS, :].bitcast(F32),
                                        ALU.subtract).then_inc(hs_lo_done, 1)

            def first_residual(g):
                dve.wait_ge(base_done, g.n + 1)
                dve.wait_ge(c_mm, g.n + 1)
                nc.vector.tensor_tensor(x1[g.parity][:], m0[:], base[:], ALU.add).then_inc(x1_done, 1)

            def z_mean_square(g):
                dve.wait_ge(ms_mm, g.n + 1)
                nc.vector.tensor_scalar(z_msq[:], m0[:, 0:TT], 1.0 / D, RMS_EPS, ALU.mult, ALU.add).then_inc(z_msq_done, 1)

            def low_part(g, s):
                k, b = hidden_rows(s), bank(g, s)
                f = (s - ES) // 2
                if s < ES:
                    dve.wait_ge(h_hi_done, g.n * ES + s + 1)
                    nc.vector.scalar_tensor_tensor(h_lo[b][:], hid[b][:], 0.0, h_hi[b][:].bitcast(F32),
                                                   ALU.max, ALU.subtract).then_inc(h_lo_done, 1)
                elif s % 2:
                    dve.wait_ge(gv_hi_done, g.n * FC + f + 1)
                    nc.vector.tensor_tensor(h_lo[b][0:k, :], gv[f % 2][0:k, :], h_hi[b][0:k, :].bitcast(F32),
                                            ALU.subtract).then_inc(gv_lo_done, 1)

            def gate_value(g, s):
                k, b = hidden_rows(s), bank(g, s)
                f = (s - ES) // 2
                dve.wait_ge(gate_done, g.n * FC + f + 1)
                dve.wait_ge(hid_mm, g.n * SLOTS + s + 1)
                nc.vector.tensor_tensor(gv[f % 2][0:k, :], hid[b][0:k, :], gate[0:k, :], ALU.mult).then_inc(gv_done, 1)

            def scale_expert(g, e):
                if e == 0:
                    passed(dve, moe_silu_done, g.n)
                elif e >= 3:
                    dve.wait_ge(moe_added, g.n * (E - 1) + e - 2)
                dve.wait_ge(s_b_done[e % 4], g.n * (E // 4 * 16) + (e // 4 + 1) * 16)
                dve.wait_ge(y_mm, g.n * YS + e + 1)
                nc.vector.scalar_tensor_tensor((ys[e % 2] if e else moe)[:], y[y_bank(g, e)][:], vecT[:, e:e + 1],
                                               s_b[e % 4][:], ALU.add, ALU.mult).then_inc(y_scaled, 1)

            def second_residual(g):
                dve.wait_ge(y_mm, g.n * YS + YS)
                nc.vector.tensor_tensor(s_sum[:], y[y_bank(g, E)][:], x1[g.parity][:], ALU.add).then_inc(s_sum_done, 1)

            def result(g):
                dve.wait_ge(sg_t, g.n + 1)
                xg = x_all[:, bass.ds(g.n, 1), :, :].rearrange("p o j d -> p (o j d)")
                nc.vector.tensor_tensor(xg, m1[:], xg, ALU.add).then_inc(out_done, 1)

            def W1_shift(k):
                experts = slice(k * PART, (k + 1) * PART)
                dve.wait_ge(W1_rest_loaded if k else W1_loaded, 32 if k else 48)
                nc.vector.tensor_tensor(W1_raw[:, experts], W1_raw[:, experts], W1_row0[:, experts],
                                        ALU.subtract).then_inc(W1_shifted, 1)

            def W1_low(k):
                experts = slice(k * PART, (k + 1) * PART)
                dve.wait_ge(W1_hi_done, k + 1)
                nc.vector.tensor_tensor(W1_lo[:, experts], W1_raw[:, experts], W1_hi[:, experts].bitcast(F32),
                                        ALU.subtract).then_inc(W1_lo_done, 1)

            def ffn_weights(i):
                dve.wait_ge(wt_t, i + 2)
                if i < 2:
                    last = nc.vector.tensor_scalar(w13T[i][:], m1[:, 0:FF], vecT[:, E + 2:E + 3], None, ALU.mult)
                else:
                    for c in range(FC):
                        k = hidden_rows(ES + 2 * c)
                        last = nc.vector.tensor_copy(w2T[0:k, c, :], m1[0:k, c * D:c * D + D])
                last.then_inc(ffn_wt, 1)

            g0 = Group(0, 0, 0)
            for piece in (statistics, statistics_sums, statistics_mean, statistics_var, statistics_eps,
                          mean_square, mean_square_var, mean_square_eps):
                piece(g0)
            W1_shift(0)
            dve.wait_ge(wt_t, 1)
            nc.vector.tensor_copy(vecT[:], hid[0][:, 0:E + 3]).then_inc(small_wt, 1)
            dve.wait_ge(small_wt, 1)
            nc.vector.tensor_tensor(D_w[:], vecT[:, E:E + 1], vecT[:, E + 1:E + 2], ALU.mult).then_inc(small_wt, 1)
            nc.vector.tensor_scalar(BT[:, 0:NS], hid[1][:, 0:NS], vecT[:, E + 1:E + 2], None, ALU.mult)
            nc.vector.tensor_copy(CT[:], hid[2][0:NS, 0:D]).then_inc(small_wt, 1)
            W1_low(0)
            dve.wait_ge(small_hi, 1)
            nc.vector.tensor_tensor(BT_lo[:], BT[:], BT_hi[:].bitcast(F32), ALU.subtract)
            nc.vector.tensor_tensor(C_stack[2 * NS:3 * NS, :], CT[:], C_stack[0:NS, :].bitcast(F32),
                                    ALU.subtract).then_inc(small_lo, 1)
            route_logits(g0)
            dve.wait_ge(route_step, 1)
            route_top(g0)
            route_index(g0)
            dve.wait_ge(lam_done, 17)
            nc.vector.tensor_scalar(lam[:], lam_tanh[:], 0.5, 0.5, ALU.mult, ALU.add).then_inc(lam_done, 1)
            dve.wait_ge(lam_done, 18)
            nc.vector.tensor_scalar(lam_b[:], lam_b[:], lam[:, 0:1], None, ALU.mult).then_inc(lam_done, 1)
            W1_shift(1)
            route_scores(g0)
            route_parts(g0)
            route_table(g0)
            low_part(g0, 0)
            scale_input(g0)
            dve.wait_ge(lam_done, 19)
            scan(g0)
            W1_low(1)
            low_part(g0, 1)
            hs_low(g0)
            W1_shift(2)
            W1_shift(3)

            def slot(g, c):
                n = after(g) if has_next(g) else None
                nxt = ahead(g, c, 2)
                if nxt and nxt[1] < ES:
                    low_part(*nxt)
                if is_first(g) and c in (0, 2):
                    W1_low(2 + c // 2)
                if is_first(g) and c % 2:
                    ffn_weights(c // 2)
                if c == 0:
                    first_residual(g)
                if c == 2:
                    z_mean_square(g)
                if c == 4 and before(g):
                    result(before(g))
                if n:
                    if c == 0:
                        statistics(n)
                    if c == 1:
                        statistics_sums(n)
                        statistics_mean(n)
                    if c == 3:
                        statistics_var(n)
                    if c == 4:
                        mean_square(n)
                    if c == 11:
                        route_logits(n)
                        dve.wait_ge(route_step, n.n * 5 + 1)
                    if c == 12:
                        route_scores(n)
                        route_index(n)
                    if c == 13:
                        route_parts(n)
                if c == 13:
                    gate_value(g, ES + 1)
                if c == 15:
                    low_part(g, ES + 1)
                    if n:
                        route_table(n)
                if c == 16:
                    gate_value(g, ES + 3)
                if c == 17:
                    if n:
                        scale_input(n)
                        scan(n)
                    low_part(g, ES + 3)
                if c == 18:
                    gate_value(g, ES + 5)
                if c in (1, 3, 5, 8, 10, 11, 13, 19):
                    scale_expert(g, (1, 3, 5, 8, 10, 11, 13, 19).index(c))
                if c == 11 and n:
                    route_top(n)
                if c == 19:
                    low_part(g, ES + 5)
                    if n:
                        hs_low(n)
                if c == 20:
                    second_residual(g)
                if n:
                    if c == 3:
                        statistics_eps(n)
                    if c == 5:
                        mean_square_var(n)
                    if c == 7:
                        mean_square_eps(n)

            iterations(dve, slot)
            last_group = Group(B - 1, B // 2 - 1, 1)
            result(last_group)

        @block.tensor
        def _(pe):
            def three(out_ap, w_hi, w_lo, v_hi, v_lo, start=True, stop=True):
                pe.matmul(out_ap, w_hi, v_hi, start=start, stop=False)
                pe.matmul(out_ap, w_hi, v_lo, start=False, stop=False)
                return pe.matmul(out_ap, w_lo, v_hi, start=False, stop=stop)

            def xn_transpose(g):
                passed(pe, r_rows_done, g.n)
                pe.wait_ge(xn_tok_done, g.n + 1)
                for j in range(TT):
                    last = pe.transpose(m0[:, j * P:(j + 1) * P], xn_tok[:, j, :], ident[:])
                last.then_inc(xn_t, 1)

            def rrms_transpose(g):
                pe.wait_ge(rrms_done, g.n + 1)
                pe.transpose(m1[0:TT, 0:P], rrms[:], ident[:]).then_inc(rrms_t, 1)

            def router(g):
                pe.wait_ge(xn_copied, g.n + 1)
                for j in range(TT):
                    last = pe.matmul(m0[:, j * E:(j + 1) * E], base[:, j * P:(j + 1) * P], Wg_raw[:], start=True, stop=True)
                last.then_inc(logits_mm, 1)

            def state_input(g):
                pe.wait_ge(rrms_rows_done, g.n + 1)
                pe.wait_ge(xn_lo_done, g.n + 1)
                three(m1[:], BT_hi[:], BT_lo[:], xn_hi[g.parity][:], xn_lo[g.parity][:]).then_inc(bu_mm, 1)

            def score_transpose(g):
                pe.wait_ge(s_tok_done, g.n + 1)
                for j in range(TT):
                    last = pe.transpose(m0[0:E, j * P:(j + 1) * P], s_tok[:, j, :], ident[:])
                last.then_inc(s_t, 1)

            def state_output(g):
                pe.wait_ge(s_row_done, g.n + 1)
                pe.wait_ge(hs_lo_done, g.n + 1)
                pe.matmul(m0[:], C_stack[:], hs_stack[:], start=True, stop=True).then_inc(c_mm, 1)

            def z_sums(g):
                pe.wait_ge(sq_done, g.n + 1)
                for j in range(TT):
                    last = pe.matmul(m0[:, j:j + 1], x1_sq[:, j * P:(j + 1) * P], ones[:, 0:1], start=True, stop=True)
                last.then_inc(ms_mm, 1)

            def r_transpose(g):
                pe.wait_ge(z_r_done, g.n + 1)
                pe.transpose(m0[0:TT, 0:P], z_r[:], ident[:]).then_inc(r_t, 1)

            def result_transpose(g):
                pe.wait_ge(sg_done, g.n + 1)
                for j in range(TT):
                    last = pe.transpose(m1[:, j * P:(j + 1) * P], sg[:, j * P:(j + 1) * P], ident[:])
                last.then_inc(sg_t, 1)

            def first_product(g, s):
                k, b = hidden_rows(s), bank(g, s)
                if s < ES:
                    if s == 0:
                        pe.wait_ge(bias_row, g.n + 1)
                    if s in (0, 2):
                        passed(pe, gate_done, g.n * FC - 1 + s // 2)
                    e, c = s // HC, s % HC
                    cols = slice(c * P, (c + 1) * P)
                    last = three(hid[b][:], W1_hi[:, e, cols], W1_lo[:, e, cols], xn_hi[g.parity][:], xn_lo[g.parity][:])
                else:
                    f, i = (s - ES) // 2, (s - ES) % 2
                    if s == ES:
                        pe.wait_ge(ffn_lo, 1)
                        pe.wait_ge(z_lo_done, g.n + 1)
                    if s == ES + 4:
                        pe.wait_ge(gate_done, g.n * FC + 1)
                    cols = slice(f * P, f * P + k)
                    last = three(hid[b][0:k, :], w13T_hi[i][:, cols], w13T_lo[i][:, cols], z_hi[:], z_lo[:])
                last.then_inc(hid_mm, 1)

            def second_product(g, s):
                k, b = hidden_rows(s), bank(g, s)
                if s < ES:
                    e, c = s // HC, s % HC
                    if c == 0:
                        if e == 1:
                            passed(pe, s_sum_done, g.n)
                        else:
                            passed(pe, y_scaled, g.n * E + (e - 1 if e else 0))
                    pe.wait_ge(h_lo_done, g.n * ES + s + 1)
                    last = three(y[y_bank(g, e)][:], W2_hi[:, e, c, :], W2_lo[:, e, c, :], h_hi[b][:], h_lo[b][:],
                                 start=(c == 0), stop=(c == HC - 1))
                    if c == HC - 1:
                        last.then_inc(y_mm, 1)
                elif s % 2:
                    f = (s - ES) // 2
                    if f == 0:
                        pe.wait_ge(y_scaled, g.n * E + E - 1)
                    pe.wait_ge(gv_lo_done, g.n * FC + f + 1)
                    last = three(y[y_bank(g, E)][:], w2T_hi[0:k, f, :], w2T_lo[0:k, f, :], h_hi[b][0:k, :], h_lo[b][0:k, :],
                                 start=(f == 0), stop=(f == FC - 1))
                    if f == FC - 1:
                        last.then_inc(y_mm, 1)

            g0 = Group(0, 0, 0)
            pe.wait_ge(ident_made, 2)
            pe.wait_ge(small_loaded, 16 * 7)
            pe.transpose(hid[0][:, 0:E + 3], vec_rows[:], ident[0:E + 3, 0:E + 3])
            pe.transpose(hid[1][:, 0:NS], Bw_raw[:], ident[0:NS, 0:NS])
            pe.transpose(hid[2][0:NS, 0:D], Cw_raw[:], ident[:]).then_inc(wt_t, 1)
            xn_transpose(g0)
            rrms_transpose(g0)
            router(g0)
            pe.wait_ge(small_lo, 1)
            state_input(g0)
            pe.wait_ge(W1_lo_done, 1)
            first_product(g0, 0)
            first_product(g0, 1)
            first_product(g0, 2)
            score_transpose(g0)
            pe.wait_ge(W2_lo_done, 1)

            def ffn_transpose(i):
                if i:
                    pe.wait_ge(ffn_wt, i)
                else:
                    pe.wait_ge(ffn_loaded, 16 * 5)
                for c in range(FC):
                    k = hidden_rows(ES + 2 * c)
                    if i < 2:
                        last = pe.transpose(m1[:, c * P:c * P + k], (w1_raw, w3_raw)[i][0:k, c, :], ident[0:k, 0:k])
                    else:
                        last = pe.transpose(m1[0:k, c * D:c * D + D], w2_raw[:, c * P:c * P + k], ident[:])
                last.then_inc(wt_t, 1)

            def slot(g, c):
                n = after(g) if has_next(g) else None
                if is_first(g) and c in (1, 5):
                    pe.wait_ge(W1_lo_done, 2 + c // 4)
                if is_first(g) and c == 4:
                    pe.wait_ge(W2_lo_done, 2)
                nxt = ahead(g, c, AHEAD)
                if nxt:
                    first_product(*nxt)
                if c == 3:
                    z_sums(g)
                if c == 3 and before(g):
                    result_transpose(before(g))
                if c == 5:
                    r_transpose(g)
                if c == 11 and n:
                    rrms_transpose(n)
                if c == 16 and n:
                    state_input(n)
                second_product(g, c)
                if c == 0:
                    state_output(g)
                if is_first(g) and c in (0, 2, 4):
                    ffn_transpose(c // 2)
                if is_first(g) and c == 5:
                    pe.wait_ge(W1_lo_done, PARTS)
                    pe.wait_ge(W2_lo_done, PARTS)
                if c == 8 and n:
                    xn_transpose(n)
                if c == 10 and n:
                    router(n)
                if c == 18 and n:
                    score_transpose(n)

            iterations(pe, slot)
            result_transpose(Group(B - 1, B // 2 - 1, 1))


_INS = ['L0_attn_x', 'L0_attn_log_lambda', 'L0_attn_B_w', 'L0_attn_C_w', 'L0_attn_D_skip', 'L0_attn_ssm_norm_w',
        'L0_attn_ffn_norm_w', 'L0_attn_w1', 'L0_attn_w2', 'L0_attn_w3', 'L0_ffn_Wg', 'L0_ffn_W1', 'L0_ffn_b1',
        'L0_ffn_W2', 'L0_ffn_b2']
_OUTS = [((B, T, D), 'float32')]


def kernel(**inputs):
    import numpy as _np
    import concourse.bacc as _bacc
    from concourse import mybir as _mybir
    from concourse.bass_utils import run_bass_kernel_spmd as _run

    nc = _bacc.Bacc("TRN2", target_bir_lowering=False, num_devices=1)
    arrays, args = {}, []
    for name in _INS:
        a = _np.ascontiguousarray(inputs[name])
        arrays[f"in_{name}_dram"] = a
        args.append(nc.dram_tensor(f"in_{name}_dram", a.shape, _mybir.dt.from_np(a.dtype), kind="ExternalInput").ap())
    for i, (shape, dtype) in enumerate(_OUTS):
        dt = _mybir.dt.from_np(_np.dtype(dtype))
        args.append(nc.dram_tensor(f"out_{i}_dram", shape, dt, kind="ExternalOutput").ap())
    build(nc, *args)
    r = _run(nc, [arrays], core_ids=[0])
    got = tuple(r.results[0][f"out_{i}_dram"] for i in range(len(_OUTS)))
    return got[0]
```

```python
from collections import namedtuple
from contextlib import ExitStack

import concourse.bass as bass
from concourse import mybir

P = 128
D = 128
B = 16
T = 512
TT = T // P
NS = 32
FF = 344
FC = (FF + P - 1) // P
E = 8
H = 256
HC = H // P
ES = E * HC
SLOTS = ES + 2 * FC
YS = E + 1
PART = 2
PARTS = E // PART
AHEAD = 3
FIRST = 6
STEPS = 6
LN_EPS = 1e-5
RMS_EPS = 1e-6
GATE = 64

F32 = mybir.dt.float32
F32R = mybir.dt.float32r
U32 = mybir.dt.uint32
ALU = mybir.AluOpType
ACT = mybir.ActivationFunctionType

Group = namedtuple("Group", "n half parity")


def after(g):
    return Group(g.n + 1, g.half + g.parity, 1 - g.parity)


def hidden_rows(s):
    return P if s < ES else min(P, FF - (s - ES) // 2 * P)


def build(nc, x, log_lambda, B_w, C_w, D_skip, ssm_norm_w, ffn_norm_w, w1, w2, w3, Wg, W1, b1, W2, b2, out):
    x_v = x.rearrange("b (j p) d -> b p j d", p=P)
    out_v = out.rearrange("b (j p) d -> b p j d", p=P)

    with ExitStack() as ctx:
        def sb(name, shape, dt=F32):
            return ctx.enter_context(nc.sbuf_tensor(name, shape, dt))

        def psum(name, shape):
            return ctx.enter_context(nc.psum_tensor(name, shape, F32))

        def sem(name):
            return ctx.enter_context(nc.semaphore(name))

        W1_raw = sb("W1_raw", [P, E, H])
        W1_row0 = sb("W1_row0", [P, E, H])
        W2_raw = sb("W2_raw", [P, E, HC, D])
        Wg_raw = sb("Wg_raw", [P, E])
        w1_raw = sb("w1_raw", [P, FC, D])
        w3_raw = sb("w3_raw", [P, FC, D])
        w2_raw = sb("w2_raw", [P, FF])
        Bw_raw = sb("Bw_raw", [NS, D])
        Cw_raw = sb("Cw_raw", [D, NS])
        vec_rows = sb("vec_rows", [E + 3, D])
        log_lam = sb("log_lam", [NS, 1])
        W1_hi, W1_lo = sb("W1_hi", [P, E, H], F32R), sb("W1_lo", [P, E, H], F32R)
        W2_hi, W2_lo = sb("W2_hi", [P, E, HC, D], F32R), sb("W2_lo", [P, E, HC, D], F32R)
        w1T, w3T = sb("w1T", [P, FF]), sb("w3T", [P, FF])
        w13T = [w1T, w3T]
        w13T_hi = [sb("w1T_hi", [P, FF], F32R), sb("w3T_hi", [P, FF], F32R)]
        w13T_lo = [sb("w1T_lo", [P, FF], F32R), sb("w3T_lo", [P, FF], F32R)]
        w2T = sb("w2T", [P, FC, D])
        w2T_hi, w2T_lo = sb("w2T_hi", [P, FC, D], F32R), sb("w2T_lo", [P, FC, D], F32R)
        in_w = sb("in_w", [P, P])
        in_hi, in_lo = sb("in_hi", [P, P], F32R), sb("in_lo", [P, P], F32R)
        CT = sb("CT", [NS, D])
        C_stack = sb("C_stack", [3 * NS, D], F32R)
        vecT = sb("vecT", [P, E + 3])
        D_w = sb("D_w", [P, 1])
        lam_tanh, lam = sb("lam_tanh", [NS, 1]), sb("lam", [NS, 1])
        lam_b = sb("lam_b", [NS, T])
        ident = sb("ident", [P, P])
        ones = sb("ones", [P, 1])
        warm = sb("warm", [P, 1])
        minus_half = sb("minus_half", [P, TT])
        expert_no = sb("expert_no", [P, TT, E])
        x_all = sb("x_all", [P, B, TT, D])
        bn = sb("bn", [P, TT, 6])
        shift = sb("shift", [P, TT])
        mean_sum, mean_gap, square_sum = sb("mean_sum", [P, TT]), sb("mean_gap", [P, TT]), sb("square_sum", [P, TT])
        mean, gap_square, var = sb("mean", [P, TT]), sb("gap_square", [P, TT]), sb("var", [P, TT])
        var_eps, rstd = sb("var_eps", [P, TT]), sb("rstd", [P, TT])
        rstd2, msq, msq_eps, rrms = sb("rstd2", [P, TT]), sb("msq", [P, TT]), sb("msq_eps", [P, TT]), sb("rrms", [P, TT])
        xn_tok = sb("xn_tok", [P, TT, D])
        xn_hi = [sb(f"xn_hi{i}", [P, T], F32R) for i in range(2)]
        xn_lo = [sb(f"xn_lo{i}", [P, T], F32R) for i in range(2)]
        rrms_rows, rrms_b = sb("rrms_rows", [TT, P]), sb("rrms_b", [P, T])
        base = sb("base", [P, T])
        skip_w = sb("skip_w", [P, T])
        logit_rows = sb("logit_rows", [P, T])
        logits = sb("logits", [P, TT, E])
        top, top_i = sb("top", [P, TT, 8]), sb("top_i", [P, TT, 8], U32)
        gap, gap_tanh = sb("gap", [P, TT]), sb("gap_tanh", [P, TT])
        score = [sb(f"score{k}", [P, TT]) for k in range(2)]
        chosen = [sb(f"chosen{k}", [P, TT, E]) for k in range(2)]
        part = [sb(f"part{k}", [P, TT, E]) for k in range(2)]
        s_tok = sb("s_tok", [P, TT, E])
        s_row = sb("s_row", [E, T])
        s_b = [sb(f"s_b{i}", [P, T]) for i in range(4)]
        bu, hs = sb("bu", [NS, T]), sb("hs", [NS, T])
        hs_stack = sb("hs_stack", [3 * NS, T], F32R)
        x1 = [sb(f"x1_{i}", [P, T]) for i in range(2)]
        x1_sq = sb("x1_sq", [P, T])
        z_msq, z_r = sb("z_msq", [P, TT]), sb("z_r", [P, TT])
        r_rows, r_b = sb("r_rows", [TT, P]), sb("r_b", [P, T])
        z = sb("z", [P, T])
        z_hi, z_lo = sb("z_hi", [P, T], F32R), sb("z_lo", [P, T], F32R)
        h_hi = [sb(f"h_hi{i}", [P, T], F32R) for i in range(4)]
        h_lo = [sb(f"h_lo{i}", [P, T], F32R) for i in range(4)]
        gate, gv = sb("gate", [P, T]), [sb(f"gv{i}", [P, T]) for i in range(2)]
        ys = [sb(f"ys{i}", [P, T]) for i in range(2)]
        moe, moe_silu = sb("moe", [P, T]), sb("moe_silu", [P, T])
        s_sum, sg = sb("s_sum", [P, T]), sb("sg", [P, T])

        hid = [psum(f"hid{i}", [P, T]) for i in range(4)]
        y = [psum(f"y{i}", [P, T]) for i in range(2)]
        m0, m1 = psum("m0", [P, T]), psum("m1", [P, T])

        x_loaded = [sem("x_even_loaded"), sem("x_odd_loaded")]
        small_loaded, ffn_loaded = sem("small_loaded"), sem("ffn_loaded")
        W1_loaded, W1_rest_loaded = sem("W1_loaded"), sem("W1_rest_loaded")
        W2_loaded, W2_rest_loaded = sem("W2_loaded"), sem("W2_rest_loaded")
        stored = sem("stored")
        row0_cleared = sem("row0_cleared")
        pool_consts, dve_consts, ident_made = sem("pool_consts"), sem("dve_consts"), sem("ident_made")
        lam_done, wt_t = sem("lam_done"), sem("wt_t")
        small_wt, small_hi, small_lo = sem("small_wt"), sem("small_hi"), sem("small_lo")
        ffn_wt, w2_wt, ffn_hi, ffn_lo = sem("ffn_wt"), sem("w2_wt"), sem("ffn_hi"), sem("ffn_lo")
        W1_shifted, W1_hi_done, W1_lo_done = sem("W1_shifted"), sem("W1_hi_done"), sem("W1_lo_done")
        W2_hi_done, W2_lo_done = sem("W2_hi_done"), sem("W2_lo_done")
        stats_step = sem("stats_step")
        var_done, shift_done, msq_done = sem("var_done"), sem("shift_done"), sem("msq_done")
        rstd_done, rrms_done = sem("rstd_done"), sem("rrms_done")
        xn_tok_done = sem("xn_tok_done")
        xn_t, rrms_t = sem("xn_t"), sem("rrms_t")
        xn_copied, xn_hi_done = sem("xn_copied"), sem("xn_hi_done")
        rrms_rows_done, rrms_b_done, skip_w_done = sem("rrms_rows_done"), sem("rrms_b_done"), sem("skip_w_done")
        xn_lo_done, base_done = sem("xn_lo_done"), sem("base_done")
        bias_row = sem("bias_row")
        bu_mm, logits_t, s_t = sem("bu_mm"), sem("logits_t"), sem("s_t")
        logit_rows_done = sem("logit_rows_done")
        route_step, gap_done, scored, s_tok_done = sem("route_step"), sem("gap_done"), sem("scored"), sem("s_tok_done")
        tanh_done, s_row_done = sem("tanh_done"), sem("s_row_done")
        s_b_done = [sem(f"s_b{i}_done") for i in range(4)]
        bu_done, hs_done, hs_lo_done, hs_hi_done = sem("bu_done"), sem("hs_done"), sem("hs_lo_done"), sem("hs_hi_done")
        c_mm, x1_done, sq_done, ms_mm = sem("c_mm"), sem("x1_done"), sem("sq_done"), sem("ms_mm")
        z_msq_done, z_r_done, r_t, r_rows_done = sem("z_msq_done"), sem("z_r_done"), sem("r_t"), sem("r_rows_done")
        r_b_done, z_done, z_hi_done, z_lo_done = sem("r_b_done"), sem("z_done"), sem("z_hi_done"), sem("z_lo_done")
        hid_mm, y_mm = sem("hid_mm"), sem("y_mm")
        h_hi_done, h_lo_done = sem("h_hi_done"), sem("h_lo_done")
        gate_done, gv_done, gv_hi_done, gv_lo_done = sem("gate_done"), sem("gv_done"), sem("gv_hi_done"), sem("gv_lo_done")
        y_scaled, moe_added = sem("y_scaled"), sem("moe_added")
        moe_silu_done, s_sum_done, sg_done, sg_t, out_done = sem("moe_silu_done"), sem("s_sum_done"), sem("sg_done"), sem("sg_t"), sem("out_done")

        def bank(g, s):
            return (g.parity * SLOTS + s) % 4

        def y_bank(g, k):
            return (g.parity * YS + k) % 2

        def passed(eng, semaphore, value):
            if not isinstance(value, int) or value > 0:
                eng.wait_ge(semaphore, value)


        def has_next(g):
            return not isinstance(g.n, int) or g.n < B - 1

        def iterations(eng, slot):
            def group(g):
                for c in range(FIRST, SLOTS):
                    slot(g, c)
                if has_next(g):
                    for c in range(FIRST):
                        slot(after(g), c)

            for c in range(FIRST):
                slot(Group(0, 0, 0), c)
            with eng.Fori(0, B // 2 - 1) as pair:
                group(Group(pair * 2, pair, 0))
                group(Group(pair * 2 + 1, pair, 1))
            group(Group(B - 2, B // 2 - 1, 0))
            group(Group(B - 1, B // 2 - 1, 1))

        def before(g):
            if isinstance(g.n, int) and g.n == 0:
                return None
            return Group(g.n - 1, g.half + g.parity - 1, 1 - g.parity)

        def ahead(g, c, by):
            if c + by < SLOTS:
                return g, c + by
            return (after(g), c + by - SLOTS) if has_next(g) else None

        def is_first(g):
            return isinstance(g.n, int) and g.n == 0

        block = ctx.enter_context(nc.Block())

        @block.sync
        def _(sp):
            def load(g):
                passed(sp, x_loaded[g.parity], g.half * 16)
                sp.dma_start(x_all[:, bass.ds(g.n, 1), :, :].rearrange("p o j d -> p (o j) d"),
                             x_v[bass.ds(g.n, 1)].rearrange("o p j d -> p (o j) d")).then_inc(x_loaded[g.parity], 16)

            def broadcast_score(g, e):
                passed(sp, y_scaled, g.n * E + e - 3)
                if e == 0:
                    sp.wait_ge(s_row_done, g.n + 1)
                sp.dma_start(s_b[e % 4][:], s_row[e:e + 1, :].unsqueeze(1).to_broadcast([1, P, T])).then_inc(s_b_done[e % 4], 16)

            def broadcast_rows(rows, to, done):
                for j in range(TT):
                    sp.dma_start(to[:, j * P:(j + 1) * P],
                                 rows[j:j + 1, :].unsqueeze(1).to_broadcast([1, P, P])).then_inc(done, 16)

            def broadcast_rrms(g):
                sp.wait_ge(rrms_rows_done, g.n + 1)
                broadcast_rows(rrms_rows, rrms_b, rrms_b_done)

            def broadcast_r(g):
                sp.wait_ge(r_rows_done, g.n + 1)
                broadcast_rows(r_rows, r_b, r_b_done)

            def store(g):
                sp.wait_ge(out_done, g.n + 1)
                sp.dma_start(out_v[bass.ds(g.n, 1)].rearrange("o p j d -> p (o j) d"),
                             x_all[:, bass.ds(g.n, 1), :, :].rearrange("p o j d -> p (o j) d")).then_inc(stored, 16)

            def load_W1(experts, done):
                n = experts.stop - experts.start
                sp.dma_start(W1_raw[1:P, experts], W1[experts, 1:P, :].rearrange("e d h -> d e h")).then_inc(done, 16)
                sp.dma_start(W1_row0[1:P, experts], W1[experts, 0:1, :].rearrange("e d h -> d e h")
                             .to_broadcast([P - 1, n, H])).then_inc(done, 16)

            def load_W2(experts, done):
                sp.dma_start(W2_raw[:, experts], W2[experts].rearrange("e (c p) d -> p e c d", p=P)).then_inc(done, 16)

            g0 = Group(0, 0, 0)
            load(g0)
            load_W1(slice(0, PART), W1_loaded)
            sp.dma_start(W1_raw[0:1], b1.rearrange("(o e) h -> o e h", o=1)).then_inc(W1_loaded, 16)
            load_W2(slice(0, PART), W2_loaded)
            sp.wait_ge(small_loaded, 16 * 7)
            load_W1(slice(PART, E), W1_rest_loaded)
            full = FF // P * P
            for w, raw in ((w1, w1_raw), (w3, w3_raw)):
                sp.dma_start(raw[:, 0:FF // P, :], w[0:full, :].rearrange("(c p) d -> p c d", p=P)).then_inc(ffn_loaded, 16)
                sp.dma_start(raw[0:FF - full, FC - 1, :], w[full:FF, :]).then_inc(ffn_loaded, 16)
            sp.dma_start(w2_raw[:], w2).then_inc(ffn_loaded, 16)
            broadcast_rrms(g0)
            load_W2(slice(PART, E), W2_rest_loaded)
            load(after(g0))

            def slot(g, c):
                if c == 1:
                    for e in range(4):
                        broadcast_score(g, e)
                if c in (2, 6, 8, 10):
                    broadcast_score(g, {2: 4, 6: 5, 8: 6, 10: 7}[c])
                if c == 4:
                    broadcast_r(g)
                if c == 5 and before(g):
                    store(before(g))
                if has_next(g):
                    if c == FIRST and not isinstance(g.n, int):
                        load(after(after(g)))
                    if c == 11:
                        broadcast_rrms(after(g))

            iterations(sp, slot)
            store(Group(B - 1, B // 2 - 1, 1))
            sp.wait_ge(stored, B * 16)

        @block.gpsimd
        def _(pool):
            nc.gpsimd.memset(ident[:], 0.0).then_inc(ident_made, 1)
            pool.wait_ge(ident_made, 1)
            nc.gpsimd.affine_select(out=ident[:], in_=ident[:], compare_op=ALU.not_equal, fill=1.0, base=0,
                                    pattern=[[-1, P]], channel_multiplier=1).then_inc(ident_made, 1)
            nc.gpsimd.memset(minus_half[:], -0.5)
            nc.gpsimd.memset(logit_rows[0:GATE, :], 0.0)
            nc.gpsimd.memset(ones[:], 1.0).then_inc(pool_consts, 1)
            pool.wait_ge(pool_consts, 1)
            nc.gpsimd.memset(W1_row0[0:1], 0.0).then_inc(row0_cleared, 1)

            def rstd_pow(g):
                pool.wait_ge(var_done, g.n + 1)
                nc.gpsimd.tensor_tensor(rstd[:], var_eps[:], minus_half[:], ALU.pow).then_inc(rstd_done, 1)

            def rrms_pow(g):
                pool.wait_ge(msq_done, g.n + 1)
                nc.gpsimd.tensor_tensor(rrms[:], msq_eps[:], minus_half[:], ALU.pow).then_inc(rrms_done, 1)

            def xn_low(g):
                pool.wait_ge(xn_hi_done, g.n + 1)
                nc.gpsimd.tensor_tensor(xn_lo[g.parity][:], base[:], xn_hi[g.parity][:].bitcast(F32),
                                        ALU.subtract).then_inc(xn_lo_done, 1)

            def bias_rows(g):
                pool.wait_ge(pool_consts, 1)
                pool.wait_ge(bu_mm, g.n + 1)
                nc.gpsimd.memset(xn_hi[g.parity][0:1, :].bitcast(F32), 1.0)
                nc.gpsimd.memset(xn_lo[g.parity][0:1, :].bitcast(F32), 0.0).then_inc(bias_row, 1)

            def skip_sum(g):
                pool.wait_ge(skip_w_done, g.n + 1)
                nc.gpsimd.tensor_tensor(base[:], base[:], skip_w[:], ALU.mult).then_inc(base_done, 1)

            def add_expert(g, e):
                if e >= 2:
                    pool.wait_ge(moe_added, g.n * (E - 1) + e - 1)
                pool.wait_ge(y_scaled, g.n * E + e + 1)
                nc.gpsimd.tensor_tensor(moe[:], moe[:], ys[e % 2][:], ALU.add).then_inc(moe_added, 1)

            def gated(g):
                pool.wait_ge(s_sum_done, g.n + 1)
                pool.wait_ge(moe_silu_done, g.n + 1)
                nc.gpsimd.tensor_tensor(sg[:], s_sum[:], moe_silu[:], ALU.mult).then_inc(sg_done, 1)

            def z_pow(g):
                pool.wait_ge(z_msq_done, g.n + 1)
                nc.gpsimd.tensor_tensor(z_r[:], z_msq[:], minus_half[:], ALU.pow).then_inc(z_r_done, 1)

            def z_scale(g):
                pool.wait_ge(r_b_done, g.n * (TT * 16) + TT * 16)
                nc.gpsimd.tensor_tensor(z[:], x1[g.parity][:], r_b[:], ALU.mult).then_inc(z_done, 1)

            def z_low(g):
                pool.wait_ge(z_hi_done, g.n + 1)
                nc.gpsimd.tensor_tensor(z_lo[:], z[:], z_hi[:].bitcast(F32), ALU.subtract).then_inc(z_lo_done, 1)

            def W2_low(k):
                experts = slice(k * PART, (k + 1) * PART)
                pool.wait_ge(W2_hi_done, k + 1)
                nc.gpsimd.tensor_tensor(W2_lo[:, experts], W2_raw[:, experts], W2_hi[:, experts].bitcast(F32),
                                        ALU.subtract).then_inc(W2_lo_done, 1)

            def w13_low(i):
                pool.wait_ge(ffn_hi, i + 1)
                nc.gpsimd.tensor_tensor(w13T_lo[i][:], w13T[i][:], w13T_hi[i][:].bitcast(F32),
                                        ALU.subtract).then_inc(ffn_lo, 1)

            def w2_low():
                pool.wait_ge(ffn_hi, 3)
                for c in range(FC):
                    k = hidden_rows(ES + 2 * c)
                    last = nc.gpsimd.tensor_tensor(w2T_lo[0:k, c, :], w2T[0:k, c, :], w2T_hi[0:k, c, :].bitcast(F32),
                                                   ALU.subtract)
                last.then_inc(ffn_lo, 1)

            g0 = Group(0, 0, 0)
            rstd_pow(g0)
            rrms_pow(g0)
            bias_rows(g0)
            W2_low(0)
            w13_low(0)

            def slot(g, c):
                n = after(g) if has_next(g) else None
                if c == 0:
                    skip_sum(g)
                    if before(g):
                        gated(before(g))
                if c == 1 and is_first(g):
                    w13_low(1)
                    W2_low(1)
                if c == 2:
                    z_pow(g)
                if c == 4:
                    if is_first(g):
                        W2_low(2)
                    if n:
                        rstd_pow(n)
                if c == 5 and is_first(g):
                    W2_low(3)
                    w2_low()
                if c == 6:
                    add_expert(g, 1)
                if c == 7 and n:
                    rrms_pow(n)
                if c == 9:
                    add_expert(g, 2)
                if c == 10:
                    z_scale(g)
                if c == 12 and n:
                    xn_low(n)
                if c == 14:
                    add_expert(g, 3)
                    z_low(g)
                if c == 15:
                    add_expert(g, 4)
                if c == 16:
                    add_expert(g, 5)
                if c == 17 and n:
                    bias_rows(n)
                if c == 18:
                    add_expert(g, 6)
                if c == 21:
                    add_expert(g, 7)

            iterations(pool, slot)

        @block.scalar
        def _(act):
            act.dma_start(Bw_raw[:], B_w).then_inc(small_loaded, 16)
            act.dma_start(vec_rows[0:E, :], b2).then_inc(small_loaded, 16)
            act.wait_ge(pool_consts, 1)
            nc.scalar.activation(warm[:], ones[:], ACT.Silu)
            for k, v in enumerate((D_skip, ssm_norm_w, ffn_norm_w)):
                act.dma_start(vec_rows[E + k:E + k + 1, :], v.rearrange("(o d) -> o d", o=1)).then_inc(small_loaded, 16)
            act.dma_start(Cw_raw[:], C_w).then_inc(small_loaded, 16)
            act.dma_start(Wg_raw[:], Wg).then_inc(small_loaded, 16)
            act.dma_start(log_lam[:], log_lambda.rearrange("(n o) -> n o", o=1)).then_inc(lam_done, 16)

            def xn_tokens(g, first):
                if first == 0:
                    act.wait_ge(pool_consts, 1)
                    act.wait_ge(shift_done, g.n + 1)
                for j in range(first, first + TT // 2):
                    last = nc.scalar.activation(
                        xn_tok[:, j, :], x_all[:, bass.ds(g.n, 1), j, :].rearrange("p o d -> p (o d)"),
                        ACT.Identity, bias=shift[:, j:j + 1], scale=rstd[:, j:j + 1])
                if first:
                    last.then_inc(xn_tok_done, 1)

            def xn_copy(g):
                act.wait_ge(xn_t, g.n + 1)
                nc.scalar.activation(base[:], m0[:], ACT.Copy).then_inc(xn_copied, 1)

            def xn_high(g):
                act.wait_ge(xn_copied, g.n + 1)
                nc.scalar.activation(xn_hi[g.parity][:], base[:], ACT.Copy).then_inc(xn_hi_done, 1)

            def rrms_to_rows(g):
                act.wait_ge(rrms_t, g.n + 1)
                nc.scalar.activation(rrms_rows[:], m1[0:TT, 0:P], ACT.Copy).then_inc(rrms_rows_done, 1)

            def skip_weight(g):
                act.wait_ge(rrms_b_done, g.n * (TT * 16) + TT * 16)
                nc.scalar.activation(skip_w[:], rrms_b[:], ACT.Identity, bias=ones[:, 0:1],
                                     scale=D_w[:, 0:1]).then_inc(skip_w_done, 1)

            def logits_to_rows(g):
                act.wait_ge(bu_mm, g.n + 1)
                nc.scalar.activation(logit_rows[GATE:P, :], m1[GATE:P, :], ACT.Copy).then_inc(logit_rows_done, 1)

            def gap_to_tanh(g):
                act.wait_ge(gap_done, g.n + 1)
                nc.scalar.activation(gap_tanh[:], gap[:], ACT.Tanh, scale=0.5).then_inc(tanh_done, 1)

            def hs_high(g):
                act.wait_ge(hs_done, g.n + 1)
                nc.scalar.activation(hs_stack[0:NS, :], hs[:], ACT.Copy)
                nc.scalar.activation(hs_stack[2 * NS:3 * NS, :], hs[:], ACT.Copy).then_inc(hs_hi_done, 1)

            def score_rows(g):
                for i in range(4):
                    passed(act, s_b_done[i], g.n * (E // 4 * 16))
                act.wait_ge(s_t, g.n + 1)
                nc.scalar.activation(s_row[:], m0[0:E, :], ACT.Copy).then_inc(s_row_done, 1)

            def square(g):
                act.wait_ge(x1_done, g.n + 1)
                nc.scalar.activation(x1_sq[:], x1[g.parity][:], ACT.Square).then_inc(sq_done, 1)

            def r_to_rows(g):
                act.wait_ge(r_t, g.n + 1)
                nc.scalar.activation(r_rows[:], m0[0:TT, 0:P], ACT.Copy).then_inc(r_rows_done, 1)

            def z_high(g):
                act.wait_ge(z_done, g.n + 1)
                nc.scalar.activation(z_hi[:], z[:], ACT.Copy).then_inc(z_hi_done, 1)

            def evacuate(g, s):
                k, b = hidden_rows(s), bank(g, s)
                f = (s - ES) // 2
                if s < ES:
                    act.wait_ge(hid_mm, g.n * SLOTS + s + 1)
                    nc.scalar.activation(h_hi[b][:], hid[b][:], ACT.Relu).then_inc(h_hi_done, 1)
                elif s % 2 == 0:
                    act.wait_ge(hid_mm, g.n * SLOTS + s + 1)
                    nc.scalar.activation(gate[0:k, :], hid[b][0:k, :], ACT.Silu).then_inc(gate_done, 1)
                else:
                    act.wait_ge(gv_done, g.n * FC + f + 1)
                    nc.scalar.activation(h_hi[b][0:k, :], gv[f % 2][0:k, :], ACT.Copy).then_inc(gv_hi_done, 1)

            def moe_gate(g):
                act.wait_ge(moe_added, g.n * (E - 1) + E - 1)
                nc.scalar.activation(moe_silu[:], moe[:], ACT.Silu).then_inc(moe_silu_done, 1)

            def W1_high(k):
                experts = slice(k * PART, (k + 1) * PART)
                act.wait_ge(W1_shifted, k + 1)
                nc.scalar.activation(W1_hi[:, experts], W1_raw[:, experts], ACT.Copy).then_inc(W1_hi_done, 1)

            def W2_high(k):
                experts = slice(k * PART, (k + 1) * PART)
                act.wait_ge(W2_rest_loaded if k else W2_loaded, 16)
                nc.scalar.activation(W2_hi[:, experts], W2_raw[:, experts], ACT.Copy).then_inc(W2_hi_done, 1)

            def w13_weights(i):
                act.wait_ge(wt_t, 2)
                nc.scalar.activation(w13T[i][:], y[i][:, 0:FF], ACT.Copy, scale=vecT[:, E + 2:E + 3]).then_inc(ffn_wt, 1)

            def w13_high(i):
                act.wait_ge(ffn_wt, i + 1)
                nc.scalar.activation(w13T_hi[i][:], w13T[i][:], ACT.Copy).then_inc(ffn_hi, 1)

            def w2_high():
                act.wait_ge(w2_wt, 1)
                for c in range(FC):
                    k = hidden_rows(ES + 2 * c)
                    last = nc.scalar.activation(w2T_hi[0:k, c, :], w2T[0:k, c, :], ACT.Copy)
                last.then_inc(ffn_hi, 1)

            g0 = Group(0, 0, 0)
            for first in (0, TT // 2):
                xn_tokens(g0, first)
            xn_copy(g0)
            act.wait_ge(small_wt, 3)
            nc.scalar.activation(in_hi[:], in_w[:], ACT.Copy).then_inc(small_hi, 1)
            xn_high(g0)
            nc.scalar.activation(C_stack[0:NS, :], CT[:], ACT.Copy)
            nc.scalar.activation(C_stack[NS:2 * NS, :], CT[:], ACT.Copy).then_inc(small_hi, 1)
            rrms_to_rows(g0)
            W1_high(0)
            act.wait_ge(lam_done, 16)
            nc.scalar.activation(lam_tanh[:], log_lam[:], ACT.Tanh, scale=0.5).then_inc(lam_done, 1)
            W2_high(0)
            logits_to_rows(g0)
            evacuate(g0, 0)
            gap_to_tanh(g0)
            evacuate(g0, 1)
            W1_high(1)
            w13_weights(0)
            w13_weights(1)
            skip_weight(g0)
            w13_high(0)
            hs_high(g0)
            score_rows(g0)
            w13_high(1)

            def slot(g, c):
                n = after(g) if has_next(g) else None
                nxt = ahead(g, c, 2)
                if nxt and nxt[1] < ES:
                    evacuate(*nxt)
                if c == 0:
                    if is_first(g):
                        W2_high(1)
                    if before(g):
                        moe_gate(before(g))
                if c == 1 and is_first(g):
                    W1_high(2)
                if c == 2:
                    if is_first(g):
                        W1_high(3)
                    square(g)
                if c == 3 and is_first(g):
                    W2_high(2)
                if c == 4 and is_first(g):
                    w2_high()
                    W2_high(3)
                if c == 5:
                    r_to_rows(g)
                if c == 6 and n:
                    xn_tokens(n, 0)
                if c == 7 and n:
                    xn_tokens(n, TT // 2)
                if c == 8 and n:
                    xn_copy(n)
                    xn_high(n)
                if c == 9 and n:
                    rrms_to_rows(n)
                if c == 10:
                    z_high(g)
                if c == 11 and n:
                    logits_to_rows(n)
                if c == 13:
                    evacuate(g, ES)
                    evacuate(g, ES + 1)
                if c == 15:
                    evacuate(g, ES + 2)
                if c == 16 and n:
                    gap_to_tanh(n)
                if c == 17:
                    if n:
                        skip_weight(n)
                    evacuate(g, ES + 3)
                if c == 18:
                    evacuate(g, ES + 4)
                    if n:
                        hs_high(n)
                if c == 19:
                    evacuate(g, ES + 5)
                if c == 21 and n:
                    score_rows(n)

            iterations(act, slot)
            moe_gate(Group(B - 1, B // 2 - 1, 1))

        @block.vector
        def _(dve):
            for e in range(E):
                nc.vector.memset(expert_no[:, :, e:e + 1], float(e))
            nc.vector.memset(in_w[:], 0.0)
            nc.vector.memset(lam_b[:], 1.0)
            nc.vector.memset(C_stack[:].bitcast(F32), 0.0).then_inc(dve_consts, 1)
            dve.wait_ge(dve_consts, 1)

            def statistics(g):
                dve.wait_ge(dve_consts, 1)
                dve.wait_ge(x_loaded[g.parity], g.half * 16 + 16)
                for j in range(TT):
                    last = nc.vector.bn_stats(bn[:, j, :], x_all[:, bass.ds(g.n, 1), j, :].rearrange("p o d -> p (o d)"))
                last.then_inc(stats_step, 1)

            def statistics_sums(g):
                half = [bn[:, :, k] for k in range(6)]
                dve.wait_ge(stats_step, g.n * STEPS + 1)
                nc.vector.tensor_tensor(mean_sum[:], half[1], half[4], ALU.add)
                nc.vector.tensor_tensor(mean_gap[:], half[1], half[4], ALU.subtract)
                nc.vector.tensor_tensor(square_sum[:], half[2], half[5], ALU.add).then_inc(stats_step, 1)

            def statistics_mean(g):
                dve.wait_ge(stats_step, g.n * STEPS + 2)
                nc.vector.tensor_scalar(mean[:], mean_sum[:], 0.5, None, ALU.mult)
                nc.vector.scalar_tensor_tensor(gap_square[:], mean_gap[:], 0.25, mean_gap[:], ALU.mult,
                                               ALU.mult).then_inc(stats_step, 1)

            def statistics_var(g):
                dve.wait_ge(stats_step, g.n * STEPS + 3)
                nc.vector.scalar_tensor_tensor(var[:], square_sum[:], 1.0 / D, gap_square[:], ALU.mult,
                                               ALU.add).then_inc(stats_step, 1)

            def statistics_eps(g):
                dve.wait_ge(stats_step, g.n * STEPS + 4)
                nc.vector.tensor_scalar(var_eps[:], var[:], LN_EPS, None, ALU.add).then_inc(var_done, 1)

            def mean_square(g):
                dve.wait_ge(rstd_done, g.n + 1)
                nc.vector.scalar_tensor_tensor(shift[:], mean[:], -1.0, rstd[:], ALU.mult, ALU.mult).then_inc(shift_done, 1)
                nc.vector.tensor_tensor(rstd2[:], rstd[:], rstd[:], ALU.mult).then_inc(stats_step, 1)

            def mean_square_var(g):
                dve.wait_ge(stats_step, g.n * STEPS + 5)
                nc.vector.tensor_tensor(msq[:], rstd2[:], var[:], ALU.mult).then_inc(stats_step, 1)

            def mean_square_eps(g):
                dve.wait_ge(stats_step, g.n * STEPS + 6)
                nc.vector.tensor_scalar(msq_eps[:], msq[:], RMS_EPS, None, ALU.add).then_inc(msq_done, 1)

            def first_xn_low(g):
                dve.wait_ge(xn_hi_done, 1)
                nc.vector.tensor_tensor(xn_lo[g.parity][:], base[:], xn_hi[g.parity][:].bitcast(F32),
                                        ALU.subtract).then_inc(xn_lo_done, 1)

            def route_logits(g):
                dve.wait_ge(logits_t, g.n + 1)
                nc.vector.tensor_copy(logits[:], m0[:].rearrange("p (j c) -> p j c", j=TT)[:, :, GATE:GATE + E]).then_inc(route_step, 1)

            def scale_input(g):
                dve.wait_ge(bu_mm, g.n + 1)
                dve.wait_ge(rrms_b_done, g.n * (TT * 16) + TT * 16)
                nc.vector.tensor_tensor(bu[:], m1[0:NS, :], rrms_b[0:NS, :], ALU.mult).then_inc(bu_done, 1)

            def scan(g):
                dve.wait_ge(bu_done, g.n + 1)
                nc.vector.tensor_tensor_scan(hs[:], lam_b[:], bu[:], 0.0, ALU.mult, ALU.add).then_inc(hs_done, 1)

            def route_top(g):
                for j in range(TT):
                    last = nc.vector.max(top[:, j, :], logits[:, j, :])
                last.then_inc(route_step, 1)
                dve.wait_ge(route_step, g.n * 5 + 2)
                nc.vector.tensor_tensor(gap[:], top[:, :, 0], top[:, :, 1], ALU.subtract).then_inc(gap_done, 1)

            def route_index(g):
                for j in range(TT):
                    last = nc.vector.max_index(top_i[:, j, :], top[:, j, :], logits[:, j, :])
                last.then_inc(route_step, 1)
                dve.wait_ge(route_step, g.n * 5 + 3)
                for k in range(2):
                    last = nc.vector.tensor_tensor(chosen[k][:], top_i[:, :, k:k + 1].to_broadcast([P, TT, E]),
                                                   expert_no[:], ALU.is_equal)
                last.then_inc(route_step, 1)

            def route_scores(g):
                dve.wait_ge(tanh_done, g.n + 1)
                for k, sign in enumerate((0.5, -0.5)):
                    last = nc.vector.tensor_scalar(score[k][:], gap_tanh[:], sign, 0.5, ALU.mult, ALU.add)
                last.then_inc(scored, 1)

            def route_parts(g):
                dve.wait_ge(route_step, g.n * 5 + 4)
                dve.wait_ge(scored, g.n + 1)
                for k in range(2):
                    last = nc.vector.tensor_tensor(part[k][:], chosen[k][:],
                                                   score[k][:].unsqueeze(2).to_broadcast([P, TT, E]), ALU.mult)
                last.then_inc(route_step, 1)

            def route_table(g):
                dve.wait_ge(route_step, g.n * 5 + 5)
                nc.vector.tensor_tensor(s_tok[:], part[0][:], part[1][:], ALU.add).then_inc(s_tok_done, 1)

            def hs_low(g):
                dve.wait_ge(hs_hi_done, g.n + 1)
                nc.vector.tensor_tensor(hs_stack[NS:2 * NS, :], hs[:], hs_stack[0:NS, :].bitcast(F32),
                                        ALU.subtract).then_inc(hs_lo_done, 1)

            def first_residual(g):
                dve.wait_ge(base_done, g.n + 1)
                dve.wait_ge(c_mm, g.n + 1)
                nc.vector.tensor_tensor(x1[g.parity][:], m0[:], base[:], ALU.add).then_inc(x1_done, 1)

            def z_mean_square(g):
                dve.wait_ge(ms_mm, g.n + 1)
                nc.vector.tensor_scalar(z_msq[:], m0[:, 0:TT], 1.0 / D, RMS_EPS, ALU.mult, ALU.add).then_inc(z_msq_done, 1)

            def low_part(g, s):
                k, b = hidden_rows(s), bank(g, s)
                f = (s - ES) // 2
                if s < ES:
                    dve.wait_ge(h_hi_done, g.n * ES + s + 1)
                    nc.vector.scalar_tensor_tensor(h_lo[b][:], hid[b][:], 0.0, h_hi[b][:].bitcast(F32),
                                                   ALU.max, ALU.subtract).then_inc(h_lo_done, 1)
                elif s % 2:
                    dve.wait_ge(gv_hi_done, g.n * FC + f + 1)
                    nc.vector.tensor_tensor(h_lo[b][0:k, :], gv[f % 2][0:k, :], h_hi[b][0:k, :].bitcast(F32),
                                            ALU.subtract).then_inc(gv_lo_done, 1)

            def gate_value(g, s):
                k, b = hidden_rows(s), bank(g, s)
                f = (s - ES) // 2
                dve.wait_ge(gate_done, g.n * FC + f + 1)
                dve.wait_ge(hid_mm, g.n * SLOTS + s + 1)
                nc.vector.tensor_tensor(gv[f % 2][0:k, :], hid[b][0:k, :], gate[0:k, :], ALU.mult).then_inc(gv_done, 1)

            def scale_expert(g, e):
                if e == 0:
                    passed(dve, moe_silu_done, g.n)
                elif e >= 3:
                    dve.wait_ge(moe_added, g.n * (E - 1) + e - 2)
                dve.wait_ge(s_b_done[e % 4], g.n * (E // 4 * 16) + (e // 4 + 1) * 16)
                dve.wait_ge(y_mm, g.n * YS + e + 1)
                nc.vector.scalar_tensor_tensor((ys[e % 2] if e else moe)[:], y[y_bank(g, e)][:], vecT[:, e:e + 1],
                                               s_b[e % 4][:], ALU.add, ALU.mult).then_inc(y_scaled, 1)

            def second_residual(g):
                dve.wait_ge(y_mm, g.n * YS + YS)
                nc.vector.tensor_tensor(s_sum[:], y[y_bank(g, E)][:], x1[g.parity][:], ALU.add).then_inc(s_sum_done, 1)

            def result(g):
                dve.wait_ge(sg_t, g.n + 1)
                xg = x_all[:, bass.ds(g.n, 1), :, :].rearrange("p o j d -> p (o j d)")
                nc.vector.tensor_tensor(xg, m1[:], xg, ALU.add).then_inc(out_done, 1)

            def W1_shift(k):
                experts = slice(k * PART, (k + 1) * PART)
                dve.wait_ge(row0_cleared, 1)
                dve.wait_ge(W1_rest_loaded if k else W1_loaded, 32 if k else 48)
                nc.vector.tensor_tensor(W1_raw[:, experts], W1_raw[:, experts], W1_row0[:, experts],
                                        ALU.subtract).then_inc(W1_shifted, 1)

            def W1_low(k):
                experts = slice(k * PART, (k + 1) * PART)
                dve.wait_ge(W1_hi_done, k + 1)
                nc.vector.tensor_tensor(W1_lo[:, experts], W1_raw[:, experts], W1_hi[:, experts].bitcast(F32),
                                        ALU.subtract).then_inc(W1_lo_done, 1)

            def w2_weights():
                dve.wait_ge(wt_t, 3)
                for c in range(FC):
                    k = hidden_rows(ES + 2 * c)
                    last = nc.vector.tensor_copy(w2T[0:k, c, :], m1[0:k, c * D:c * D + D])
                last.then_inc(w2_wt, 1)

            g0 = Group(0, 0, 0)
            for piece in (statistics, statistics_sums, statistics_mean, statistics_var, statistics_eps,
                          mean_square, mean_square_var, mean_square_eps):
                piece(g0)
            W1_shift(0)
            dve.wait_ge(wt_t, 1)
            nc.vector.tensor_copy(vecT[:], hid[0][:, 0:E + 3]).then_inc(small_wt, 1)
            dve.wait_ge(small_wt, 1)
            dve.wait_ge(small_loaded, 16 * 7)
            nc.vector.tensor_tensor(D_w[:], vecT[:, E:E + 1], vecT[:, E + 1:E + 2], ALU.mult).then_inc(small_wt, 1)
            nc.vector.tensor_copy(in_w[:, GATE:GATE + E], Wg_raw[:])
            nc.vector.tensor_scalar(in_w[:, 0:NS], hid[1][:, 0:NS], vecT[:, E + 1:E + 2], None, ALU.mult)
            nc.vector.tensor_copy(CT[:], hid[2][0:NS, 0:D]).then_inc(small_wt, 1)
            dve.wait_ge(small_hi, 1)
            nc.vector.tensor_tensor(in_lo[:], in_w[:], in_hi[:].bitcast(F32), ALU.subtract).then_inc(small_lo, 1)
            first_xn_low(g0)
            dve.wait_ge(small_hi, 2)
            nc.vector.tensor_tensor(C_stack[2 * NS:3 * NS, :], CT[:], C_stack[0:NS, :].bitcast(F32),
                                    ALU.subtract).then_inc(small_lo, 1)
            W1_low(0)
            dve.wait_ge(lam_done, 17)
            nc.vector.tensor_scalar(lam[:], lam_tanh[:], 0.5, 0.5, ALU.mult, ALU.add).then_inc(lam_done, 1)
            dve.wait_ge(lam_done, 18)
            nc.vector.tensor_scalar(lam_b[:], lam_b[:], lam[:, 0:1], None, ALU.mult).then_inc(lam_done, 1)
            route_logits(g0)
            dve.wait_ge(route_step, 1)
            route_top(g0)
            route_index(g0)
            low_part(g0, 0)
            W1_shift(1)
            route_scores(g0)
            route_parts(g0)
            route_table(g0)
            low_part(g0, 1)
            dve.wait_ge(lam_done, 19)
            scale_input(g0)
            scan(g0)
            W1_low(1)
            W1_shift(2)
            hs_low(g0)
            W1_shift(3)

            def slot(g, c):
                n = after(g) if has_next(g) else None
                nxt = ahead(g, c, 2)
                if nxt and nxt[1] < ES:
                    low_part(*nxt)
                if c == 0:
                    if before(g):
                        second_residual(before(g))
                    first_residual(g)
                    if n:
                        statistics(n)
                if c == 1:
                    if is_first(g):
                        W1_low(2)
                    if n:
                        statistics_sums(n)
                        statistics_mean(n)
                        statistics_var(n)
                if c == 2:
                    if is_first(g):
                        W1_low(3)
                    z_mean_square(g)
                    if n:
                        statistics_eps(n)
                    scale_expert(g, 0)
                if c == 3:
                    if is_first(g):
                        w2_weights()
                    scale_expert(g, 1)
                if c == 4:
                    if n:
                        mean_square(n)
                    if before(g):
                        result(before(g))
                if c == 5:
                    if n:
                        mean_square_var(n)
                    scale_expert(g, 2)
                    if n:
                        mean_square_eps(n)
                if c == 7:
                    scale_expert(g, 3)
                if c == 9:
                    scale_expert(g, 4)
                if c == 10:
                    scale_expert(g, 5)
                if c == 11 and n:
                    scale_input(n)
                if c == 13:
                    scale_expert(g, 6)
                    gate_value(g, ES + 1)
                if c == 14 and n:
                    route_logits(n)
                    dve.wait_ge(route_step, n.n * 5 + 1)
                    scan(n)
                    route_top(n)
                if c == 15:
                    low_part(g, ES + 1)
                    gate_value(g, ES + 3)
                if c == 16:
                    if n:
                        route_index(n)
                        route_scores(n)
                    low_part(g, ES + 3)
                if c == 17:
                    gate_value(g, ES + 5)
                    if n:
                        route_parts(n)
                        route_table(n)
                if c == 18:
                    scale_expert(g, 7)
                if c == 19:
                    low_part(g, ES + 5)
                    if n:
                        hs_low(n)

            iterations(dve, slot)
            last_group = Group(B - 1, B // 2 - 1, 1)
            second_residual(last_group)
            dve.wait_ge(s_sum_done, B)
            dve.wait_ge(moe_silu_done, B)
            nc.vector.tensor_tensor(sg[:], s_sum[:], moe_silu[:], ALU.mult).then_inc(sg_done, 1)
            result(last_group)

        @block.tensor
        def _(pe):
            def three(out_ap, w_hi, w_lo, v_hi, v_lo, start=True, stop=True):
                pe.matmul(out_ap, w_hi, v_hi, start=start, stop=False)
                pe.matmul(out_ap, w_hi, v_lo, start=False, stop=False)
                return pe.matmul(out_ap, w_lo, v_hi, start=False, stop=stop)

            def xn_transpose(g):
                passed(pe, r_rows_done, g.n)
                pe.wait_ge(xn_tok_done, g.n + 1)
                for j in range(TT):
                    last = pe.transpose(m0[:, j * P:(j + 1) * P], xn_tok[:, j, :], ident[:])
                last.then_inc(xn_t, 1)

            def rrms_transpose(g):
                pe.wait_ge(rrms_done, g.n + 1)
                pe.transpose(m1[0:TT, 0:P], rrms[:], ident[:]).then_inc(rrms_t, 1)

            def logit_transpose(g):
                pe.wait_ge(xn_copied, g.n + 1)
                pe.wait_ge(logit_rows_done, g.n + 1)
                for j in range(TT):
                    last = pe.transpose(m0[:, j * P:(j + 1) * P], logit_rows[:, j * P:(j + 1) * P], ident[:])
                last.then_inc(logits_t, 1)

            def state_input(g):
                pe.wait_ge(rrms_rows_done, g.n + 1)
                pe.wait_ge(xn_lo_done, g.n + 1)
                three(m1[:], in_hi[:], in_lo[:], xn_hi[g.parity][:], xn_lo[g.parity][:]).then_inc(bu_mm, 1)

            def score_transpose(g):
                pe.wait_ge(s_tok_done, g.n + 1)
                for j in range(TT):
                    last = pe.transpose(m0[0:E, j * P:(j + 1) * P], s_tok[:, j, :], ident[:])
                last.then_inc(s_t, 1)

            def state_output(g):
                pe.wait_ge(s_row_done, g.n + 1)
                pe.wait_ge(hs_lo_done, g.n + 1)
                pe.matmul(m0[:], C_stack[:], hs_stack[:], start=True, stop=True).then_inc(c_mm, 1)

            def z_sums(g):
                pe.wait_ge(sq_done, g.n + 1)
                for j in range(TT):
                    last = pe.matmul(m0[:, j:j + 1], x1_sq[:, j * P:(j + 1) * P], ones[:, 0:1], start=True, stop=True)
                last.then_inc(ms_mm, 1)

            def r_transpose(g):
                pe.wait_ge(z_r_done, g.n + 1)
                pe.transpose(m0[0:TT, 0:P], z_r[:], ident[:]).then_inc(r_t, 1)

            def result_transpose(g):
                pe.wait_ge(sg_done, g.n + 1)
                for j in range(TT):
                    last = pe.transpose(m1[:, j * P:(j + 1) * P], sg[:, j * P:(j + 1) * P], ident[:])
                last.then_inc(sg_t, 1)

            def first_product(g, s):
                k, b = hidden_rows(s), bank(g, s)
                if s < ES:
                    if s == 0:
                        pe.wait_ge(bias_row, g.n + 1)
                    if s in (0, 2):
                        passed(pe, gate_done, g.n * FC - 1 + s // 2)
                    e, c = s // HC, s % HC
                    cols = slice(c * P, (c + 1) * P)
                    last = three(hid[b][:], W1_hi[:, e, cols], W1_lo[:, e, cols], xn_hi[g.parity][:], xn_lo[g.parity][:])
                else:
                    f, i = (s - ES) // 2, (s - ES) % 2
                    if s == ES:
                        pe.wait_ge(ffn_lo, 3)
                        pe.wait_ge(z_lo_done, g.n + 1)
                    if s == ES + 4:
                        pe.wait_ge(gate_done, g.n * FC + 1)
                    cols = slice(f * P, f * P + k)
                    last = three(hid[b][0:k, :], w13T_hi[i][:, cols], w13T_lo[i][:, cols], z_hi[:], z_lo[:])
                last.then_inc(hid_mm, 1)

            def second_product(g, s):
                k, b = hidden_rows(s), bank(g, s)
                if s < ES:
                    e, c = s // HC, s % HC
                    if c == 0:
                        if e == 1:
                            passed(pe, s_sum_done, g.n)
                        else:
                            passed(pe, y_scaled, g.n * E + (e - 1 if e else 0))
                    if s == (PARTS - 1) * PART * HC:
                        pe.wait_ge(W2_lo_done, PARTS)
                    pe.wait_ge(h_lo_done, g.n * ES + s + 1)
                    last = three(y[y_bank(g, e)][:], W2_hi[:, e, c, :], W2_lo[:, e, c, :], h_hi[b][:], h_lo[b][:],
                                 start=(c == 0), stop=(c == HC - 1))
                    if c == HC - 1:
                        last.then_inc(y_mm, 1)
                elif s % 2:
                    f = (s - ES) // 2
                    if f == 0:
                        pe.wait_ge(y_scaled, g.n * E + E - 1)
                    pe.wait_ge(gv_lo_done, g.n * FC + f + 1)
                    last = three(y[y_bank(g, E)][:], w2T_hi[0:k, f, :], w2T_lo[0:k, f, :], h_hi[b][0:k, :], h_lo[b][0:k, :],
                                 start=(f == 0), stop=(f == FC - 1))
                    if f == FC - 1:
                        last.then_inc(y_mm, 1)

            def keep_busy(n):
                for _ in range(n):
                    pe.transpose(hid[3][:, 0:P], ident[:], ident[:])

            g0 = Group(0, 0, 0)
            pe.wait_ge(ident_made, 2)
            keep_busy(24)
            pe.wait_ge(small_loaded, 16 * 7)
            pe.transpose(hid[0][:, 0:E + 3], vec_rows[:], ident[0:E + 3, 0:E + 3])
            pe.transpose(hid[1][:, 0:NS], Bw_raw[:], ident[0:NS, 0:NS])
            pe.transpose(hid[2][0:NS, 0:D], Cw_raw[:], ident[:]).then_inc(wt_t, 1)
            xn_transpose(g0)
            rrms_transpose(g0)
            keep_busy(12)
            pe.wait_ge(small_lo, 1)
            state_input(g0)
            logit_transpose(g0)
            pe.wait_ge(W1_lo_done, 1)
            first_product(g0, 0)
            first_product(g0, 1)
            first_product(g0, 2)
            pe.wait_ge(ffn_loaded, 16 * 5)
            for i, raw in enumerate((w1_raw, w3_raw)):
                for c in range(FC):
                    k = hidden_rows(ES + 2 * c)
                    last = pe.transpose(y[i][:, c * P:c * P + k], raw[0:k, c, :], ident[0:k, 0:k])
            last.then_inc(wt_t, 1)

            def w2_transpose():
                for c in range(FC):
                    k = hidden_rows(ES + 2 * c)
                    last = pe.transpose(m1[0:k, c * D:c * D + D], w2_raw[:, c * P:c * P + k], ident[:])
                last.then_inc(wt_t, 1)

            def slot(g, c):
                n = after(g) if has_next(g) else None
                if is_first(g) and c in (1, 5):
                    pe.wait_ge(W1_lo_done, 2 + c // 4)
                if is_first(g) and c == 4:
                    pe.wait_ge(W2_lo_done, 2)
                nxt = ahead(g, c, AHEAD)
                if nxt:
                    first_product(*nxt)
                if c == 3:
                    z_sums(g)
                if c == 8 and n:
                    xn_transpose(n)
                if c == 9 and n:
                    rrms_transpose(n)
                if c == 14 and n:
                    logit_transpose(n)
                if c == 0 and is_first(g):
                    pe.wait_ge(W2_lo_done, 1)
                    pe.wait_ge(ffn_wt, 1)
                second_product(g, c)
                if c == 0:
                    if is_first(g):
                        score_transpose(g)
                    else:
                        state_output(g)
                if c == 1 and is_first(g):
                    state_output(g)
                    w2_transpose()
                    pe.wait_ge(ffn_wt, 2)
                if c == 3 and before(g):
                    result_transpose(before(g))
                if c == 4:
                    r_transpose(g)
                if c == 5 and is_first(g):
                    pe.wait_ge(W1_lo_done, PARTS)
                    pe.wait_ge(W2_lo_done, PARTS - 1)
                if c == 11 and n:
                    state_input(n)
                if c == 20 and n:
                    score_transpose(n)

            iterations(pe, slot)
            result_transpose(Group(B - 1, B // 2 - 1, 1))


_INS = ['L0_attn_x', 'L0_attn_log_lambda', 'L0_attn_B_w', 'L0_attn_C_w', 'L0_attn_D_skip', 'L0_attn_ssm_norm_w',
        'L0_attn_ffn_norm_w', 'L0_attn_w1', 'L0_attn_w2', 'L0_attn_w3', 'L0_ffn_Wg', 'L0_ffn_W1', 'L0_ffn_b1',
        'L0_ffn_W2', 'L0_ffn_b2']
_OUTS = [((B, T, D), 'float32')]


def kernel(**inputs):
    import numpy as _np
    import concourse.bacc as _bacc
    from concourse import mybir as _mybir
    from concourse.bass_utils import run_bass_kernel_spmd as _run

    nc = _bacc.Bacc("TRN2", target_bir_lowering=False, num_devices=1)
    arrays, args = {}, []
    for name in _INS:
        a = _np.ascontiguousarray(inputs[name])
        arrays[f"in_{name}_dram"] = a
        args.append(nc.dram_tensor(f"in_{name}_dram", a.shape, _mybir.dt.from_np(a.dtype), kind="ExternalInput").ap())
    for i, (shape, dtype) in enumerate(_OUTS):
        dt = _mybir.dt.from_np(_np.dtype(dtype))
        args.append(nc.dram_tensor(f"out_{i}_dram", shape, dt, kind="ExternalOutput").ap())
    build(nc, *args)
    r = _run(nc, [arrays], core_ids=[0])
    got = tuple(r.results[0][f"out_{i}_dram"] for i in range(len(_OUTS)))
    return got[0]
```
